# Optimizing a Trainium2 kernel written in Bass

```python
import numpy as np
import jax
import jax.numpy as jnp

def _softmax(x, axis=-1):
    return jax.nn.softmax(x, axis=axis)

def _gelu(x):
    return jax.nn.gelu(x, approximate=True)

def _silu(x):
    return jax.nn.silu(x)

def _sigmoid(x):
    return jax.nn.sigmoid(x)

def _layernorm(x, axis=-1, eps=1e-05):
    m = jnp.mean(x, axis=axis, keepdims=True)
    v = jnp.var(x, axis=axis, keepdims=True)
    return (x - m) / jnp.sqrt(v + eps)

def _scatter_add(tgt, idx, src, axis=0):
    return tgt.at[idx].add(src)

def _segment_sum(src, seg, n):
    return jax.ops.segment_sum(src, seg, n)
kernel_name = 'mk_xattn_ffn_d2_seqx_r8_555998'

def setup_inputs(seed: int=0):
    np.random.seed(seed)
    _w = jnp.asarray

    def _rec_inputs():
        import jax
        import jax.numpy as jnp
        _rk = jax.random.key(seed)
        x = 7.22e-05 + 1 * jax.random.normal(jax.random.fold_in(_rk, 1), (4, 256, 128), jnp.float32)
        _lenS = 256 - jax.random.randint(jax.random.fold_in(_rk, 7), (4,), 0, max(1, 256 // 4) + 1, jnp.int32)
        _lenS2 = 256 - jax.random.randint(jax.random.fold_in(_rk, 8), (4,), 0, max(1, 256 // 4) + 1, jnp.int32)
        _ctx_1024P = jax.random.normal(jax.random.fold_in(_rk, 11), (4, 16, 128), jnp.float32)
        _ctx_1024c = jax.random.dirichlet(jax.random.fold_in(_rk, 511), 0.3 * jnp.ones((16,), jnp.float32), (4, 256))
        _ctx_1024t = jnp.einsum('bsk,bkd->bsd', _ctx_1024c, _ctx_1024P)
        _ctx_1024t = _ctx_1024t * jax.lax.rsqrt(jnp.mean(jnp.square(_ctx_1024t)) + 1e-12) * 0.953939
        ctx_1024 = 4.13588e-05 + 0.999923 * (_ctx_1024t + 0.3 * jax.random.normal(jax.random.fold_in(_rk, 611), (4, 256, 128), jnp.float32))
        return (x, ctx_1024)
    x, ctx_1024 = _rec_inputs()

    def _L0_xattn_setup():
        import jax, jax.numpy as jnp
        import numpy as np
        HID = 128
        HEADS = 16

        def _split_heads(x, h):
            b, s, d = x.shape
            return x.reshape(b, s, h, d // h).transpose(0, 2, 1, 3)
        key = jax.random.key(seed)
        ks = jax.random.split(key, 10)
        s = 0.02
        return {'x1': jax.random.normal(ks[0], (4, 256, HID), jnp.float32), 'x2': jax.random.normal(ks[1], (4, 256, HID), jnp.float32), 'Wq': jax.random.normal(ks[2], (HID, HID), jnp.float32) * s, 'bq': jnp.zeros((HID,), jnp.float32), 'Wk': jax.random.normal(ks[3], (HID, HID), jnp.float32) * s, 'bk': jnp.zeros((HID,), jnp.float32), 'Wv': jax.random.normal(ks[4], (HID, HID), jnp.float32) * s, 'bv': jnp.zeros((HID,), jnp.float32), 'Wo': jax.random.normal(ks[5], (HID, HID), jnp.float32) * s, 'bo': jnp.zeros((HID,), jnp.float32)}
    _L0_xattn_all = _L0_xattn_setup()
    _L0_xattn_in = {k: v for k, v in _L0_xattn_all.items() if k in ('Wq', 'bq', 'Wk', 'bk', 'Wv', 'bv', 'Wo', 'bo')}
    del _L0_xattn_all

    def _L0_ffn_setup():
        import jax, jax.numpy as jnp
        import numpy as np
        D_MODEL = 128
        EXPANSION = 4
        D_HIDDEN = D_MODEL * EXPANSION
        NUM_STAGES = int(np.log2(D_HIDDEN))

        def butterfly(y, weights, dim):
            lead = y.shape[:-1]
            for stage in range(weights.shape[0]):
                s = 2 ** stage
                nb = dim // (2 * s)
                yr = y.reshape(*lead, nb, 2, s)
                a = yr[..., 0, :]
                b = yr[..., 1, :]
                w = weights[stage].reshape(nb, s, 2, 2)
                na = w[..., 0, 0] * a + w[..., 0, 1] * b
                nb2 = w[..., 1, 0] * a + w[..., 1, 1] * b
                y = jnp.stack([na, nb2], axis=-2).reshape(*lead, dim)
            return y
        key = jax.random.key(seed)
        ks = jax.random.split(key, 6)
        B, S = (4, 256)
        x = jax.random.normal(ks[0], (B, S, D_MODEL), jnp.float32)
        W_exp = jax.random.normal(ks[1], (D_MODEL, D_HIDDEN), jnp.float32) * 0.02
        b_exp = jnp.zeros((D_HIDDEN,), jnp.float32)
        up_weights = jax.random.normal(ks[2], (NUM_STAGES, D_HIDDEN // 2, 2, 2), jnp.float32) * 0.02
        up_bias = jnp.zeros((D_HIDDEN,), jnp.float32)
        down_weights = jax.random.normal(ks[3], (NUM_STAGES, D_HIDDEN // 2, 2, 2), jnp.float32) * 0.02
        W_con = jax.random.normal(ks[4], (D_HIDDEN, D_MODEL), jnp.float32) * 0.02
        b_con = jnp.zeros((D_MODEL,), jnp.float32)
        down_bias = jnp.zeros((D_MODEL,), jnp.float32)
        return dict(x=x, W_exp=W_exp, b_exp=b_exp, up_weights=up_weights, up_bias=up_bias, down_weights=down_weights, W_con=W_con, b_con=b_con, down_bias=down_bias)
    _L0_ffn_all = _L0_ffn_setup()
    _L0_ffn_in = {k: v for k, v in _L0_ffn_all.items() if k in ('W_exp', 'b_exp', 'up_weights', 'up_bias', 'down_weights', 'W_con', 'b_con', 'down_bias')}
    del _L0_ffn_all

    def _L1_xattn_setup():
        import jax, jax.numpy as jnp
        import numpy as np
        D_MODEL = 128
        N_HEADS = 16
        HEAD_DIM = D_MODEL // N_HEADS
        SCALE = HEAD_DIM ** (-0.5)
        key = jax.random.key(seed)
        ks = jax.random.split(key, 11)
        B, L = (4, 256)
        s = 1.0 / np.sqrt(D_MODEL)
        inp = {'queries': jax.random.normal(ks[0], (B, L, D_MODEL), jnp.float32), 'keys': jax.random.normal(ks[1], (B, L, D_MODEL), jnp.float32), 'values': jax.random.normal(ks[2], (B, L, D_MODEL), jnp.float32), 'Wq': jax.random.normal(ks[3], (D_MODEL, D_MODEL), jnp.float32) * s, 'bq': jnp.zeros((D_MODEL,), jnp.float32), 'Wk': jax.random.normal(ks[4], (D_MODEL, D_MODEL), jnp.float32) * s, 'bk': jnp.zeros((D_MODEL,), jnp.float32), 'Wv': jax.random.normal(ks[5], (D_MODEL, D_MODEL), jnp.float32) * s, 'bv': jnp.zeros((D_MODEL,), jnp.float32), 'Wo': jax.random.normal(ks[6], (D_MODEL, D_MODEL), jnp.float32) * s, 'bo': jnp.zeros((D_MODEL,), jnp.float32)}
        return inp
    _L1_xattn_all = _L1_xattn_setup()
    _L1_xattn_in = {k: v for k, v in _L1_xattn_all.items() if k in ('Wq', 'bq', 'Wk', 'bk', 'Wv', 'bv', 'Wo', 'bo')}
    del _L1_xattn_all

    def _L1_ffn_setup():
        import jax, jax.numpy as jnp
        import numpy as np
        from jax import lax
        DIM = 128
        INTER = 64
        N_EXPERTS = 16
        TOPK = 4
        ROUTE_SCALE = 2.5
        VOCAB = 4000

        def _silu_and_mul(gu):
            gate, up = jnp.split(gu, 2, axis=-1)
            return jax.nn.silu(gate) * up
        key = jax.random.key(seed)
        ks = jax.random.split(key, 8)
        x = jax.random.normal(ks[0], (2, 64, DIM), dtype=jnp.float32)
        input_ids = jax.random.randint(ks[1], (2, 64), 0, VOCAB)
        s = 0.02
        gate_w = jax.random.normal(ks[2], (N_EXPERTS, DIM), dtype=jnp.float32) * s
        gate_b = jax.random.normal(ks[3], (N_EXPERTS,), dtype=jnp.float32) * s
        w13 = jax.random.normal(ks[4], (N_EXPERTS, 2 * INTER, DIM), dtype=jnp.float32) * s
        w2 = jax.random.normal(ks[5], (N_EXPERTS, DIM, INTER), dtype=jnp.float32) * s
        w13_s = jax.random.normal(ks[6], (2 * INTER, DIM), dtype=jnp.float32) * s
        w2_s = jax.random.normal(ks[7], (DIM, INTER), dtype=jnp.float32) * s
        return {'x': x, 'input_ids': input_ids, 'gate_w': gate_w, 'gate_b': gate_b, 'w13': w13, 'w2': w2, 'w13_s': w13_s, 'w2_s': w2_s}
    _L1_ffn_all = _L1_ffn_setup()
    _L1_ffn_in = {k: v for k, v in _L1_ffn_all.items() if k in ('input_ids', 'gate_w', 'gate_b', 'w13', 'w2', 'w13_s', 'w2_s')}
    del _L1_ffn_all
    return {'x': x, 'ctx_1024': ctx_1024, 'L0_xattn_Wq': _L0_xattn_in['Wq'], 'L0_xattn_bq': _L0_xattn_in['bq'], 'L0_xattn_Wk': _L0_xattn_in['Wk'], 'L0_xattn_bk': _L0_xattn_in['bk'], 'L0_xattn_Wv': _L0_xattn_in['Wv'], 'L0_xattn_bv': _L0_xattn_in['bv'], 'L0_xattn_Wo': _L0_xattn_in['Wo'], 'L0_xattn_bo': _L0_xattn_in['bo'], 'L0_ffn_W_exp': _L0_ffn_in['W_exp'], 'L0_ffn_b_exp': _L0_ffn_in['b_exp'], 'L0_ffn_up_weights': _L0_ffn_in['up_weights'], 'L0_ffn_up_bias': _L0_ffn_in['up_bias'], 'L0_ffn_down_weights': _L0_ffn_in['down_weights'], 'L0_ffn_W_con': _L0_ffn_in['W_con'], 'L0_ffn_b_con': _L0_ffn_in['b_con'], 'L0_ffn_down_bias': _L0_ffn_in['down_bias'], 'L1_xattn_Wq': _L1_xattn_in['Wq'], 'L1_xattn_bq': _L1_xattn_in['bq'], 'L1_xattn_Wk': _L1_xattn_in['Wk'], 'L1_xattn_bk': _L1_xattn_in['bk'], 'L1_xattn_Wv': _L1_xattn_in['Wv'], 'L1_xattn_bv': _L1_xattn_in['bv'], 'L1_xattn_Wo': _L1_xattn_in['Wo'], 'L1_xattn_bo': _L1_xattn_in['bo'], 'L1_ffn_input_ids': _L1_ffn_in['input_ids'], 'L1_ffn_gate_w': _L1_ffn_in['gate_w'], 'L1_ffn_gate_b': _L1_ffn_in['gate_b'], 'L1_ffn_w13': _L1_ffn_in['w13'], 'L1_ffn_w2': _L1_ffn_in['w2'], 'L1_ffn_w13_s': _L1_ffn_in['w13_s'], 'L1_ffn_w2_s': _L1_ffn_in['w2_s']}

def reference(x, ctx_1024, L0_xattn_Wq, L0_xattn_bq, L0_xattn_Wk, L0_xattn_bk, L0_xattn_Wv, L0_xattn_bv, L0_xattn_Wo, L0_xattn_bo, L0_ffn_W_exp, L0_ffn_b_exp, L0_ffn_up_weights, L0_ffn_up_bias, L0_ffn_down_weights, L0_ffn_W_con, L0_ffn_b_con, L0_ffn_down_bias, L1_xattn_Wq, L1_xattn_bq, L1_xattn_Wk, L1_xattn_bk, L1_xattn_Wv, L1_xattn_bv, L1_xattn_Wo, L1_xattn_bo, L1_ffn_input_ids, L1_ffn_gate_w, L1_ffn_gate_b, L1_ffn_w13, L1_ffn_w2, L1_ffn_w13_s, L1_ffn_w2_s):
    import jax
    import jax.numpy as jnp

    def _L0_xattn_ref(x1, x2, Wq, bq, Wk, bk, Wv, bv, Wo, bo):
        import jax, jax.numpy as jnp
        import numpy as np
        HID = 128
        HEADS = 16

        def _split_heads(x, h):
            b, s, d = x.shape
            return x.reshape(b, s, h, d // h).transpose(0, 2, 1, 3)
        q = _split_heads(x1 @ Wq.T + bq, HEADS)
        k = _split_heads(x2 @ Wk.T + bk, HEADS)
        v = _split_heads(x2 @ Wv.T + bv, HEADS)
        dh = q.shape[-1]
        scores = jnp.einsum('bhqd,bhkd->bhqk', q, k) / jnp.sqrt(jnp.float32(dh))
        attn = jax.nn.softmax(scores, axis=-1)
        out = jnp.einsum('bhqk,bhkd->bhqd', attn, v)
        b, h, sq, _ = out.shape
        out = out.transpose(0, 2, 1, 3).reshape(b, sq, h * dh)
        return out @ Wo.T + bo

    def _L0_ffn_ref(x, W_exp, b_exp, up_weights, up_bias, down_weights, W_con, b_con, down_bias):
        import jax, jax.numpy as jnp
        import numpy as np
        D_MODEL = 128
        EXPANSION = 4
        D_HIDDEN = D_MODEL * EXPANSION
        NUM_STAGES = int(np.log2(D_HIDDEN))

        def butterfly(y, weights, dim):
            lead = y.shape[:-1]
            for stage in range(weights.shape[0]):
                s = 2 ** stage
                nb = dim // (2 * s)
                yr = y.reshape(*lead, nb, 2, s)
                a = yr[..., 0, :]
                b = yr[..., 1, :]
                w = weights[stage].reshape(nb, s, 2, 2)
                na = w[..., 0, 0] * a + w[..., 0, 1] * b
                nb2 = w[..., 1, 0] * a + w[..., 1, 1] * b
                y = jnp.stack([na, nb2], axis=-2).reshape(*lead, dim)
            return y
        h = jnp.einsum('bsd,dh->bsh', x, W_exp) + b_exp
        h = butterfly(h, up_weights, D_HIDDEN)
        h = jax.nn.gelu(h + up_bias, approximate=False)
        h = butterfly(h, down_weights, D_HIDDEN)
        y = jnp.einsum('bsh,hd->bsd', h, W_con) + b_con
        return y + down_bias

    def _L1_xattn_ref(queries, keys, values, Wq, bq, Wk, bk, Wv, bv, Wo, bo):
        import jax, jax.numpy as jnp
        import numpy as np
        D_MODEL = 128
        N_HEADS = 16
        HEAD_DIM = D_MODEL // N_HEADS
        SCALE = HEAD_DIM ** (-0.5)
        B, L, _ = queries.shape
        S = keys.shape[1]
        q = (queries @ Wq + bq).reshape(B, L, N_HEADS, HEAD_DIM).transpose(0, 2, 1, 3)
        k = (keys @ Wk + bk).reshape(B, S, N_HEADS, HEAD_DIM).transpose(0, 2, 1, 3)
        v = (values @ Wv + bv).reshape(B, S, N_HEADS, HEAD_DIM).transpose(0, 2, 1, 3)
        scores = jnp.einsum('bhld,bhsd->bhls', q, k) * SCALE
        weights = jax.nn.softmax(scores, axis=-1)
        out = jnp.einsum('bhls,bhsd->bhld', weights, v)
        out = out.transpose(0, 2, 1, 3).reshape(B, L, D_MODEL)
        out = out @ Wo + bo
        return out

    def _L1_ffn_ref(x, input_ids, gate_w, gate_b, w13, w2, w13_s, w2_s):
        import jax, jax.numpy as jnp
        import numpy as np
        from jax import lax
        DIM = 128
        INTER = 64
        N_EXPERTS = 16
        TOPK = 4
        ROUTE_SCALE = 2.5
        VOCAB = 4000

        def _silu_and_mul(gu):
            gate, up = jnp.split(gu, 2, axis=-1)
            return jax.nn.silu(gate) * up
        B, S, D = x.shape
        xt = x.reshape(-1, D)
        T = xt.shape[0]
        scores = jax.nn.sigmoid(xt.astype(jnp.float32) @ gate_w.T)
        biased = scores + gate_b
        _, idx = lax.top_k(biased, TOPK)
        w = jnp.take_along_axis(scores, idx, axis=-1)
        w = w / jnp.sum(w, axis=-1, keepdims=True)
        w = w * ROUTE_SCALE
        comb = jnp.zeros((T, N_EXPERTS), jnp.float32)
        comb = comb.at[jnp.arange(T)[:, None], idx].add(w)
        comb = comb.astype(x.dtype)

        def expert_body(y, args):
            w13_e, w2_e, c_e = args
            h = _silu_and_mul(xt @ w13_e.T)
            return (y + c_e[:, None] * (h @ w2_e.T), None)
        y, _ = lax.scan(expert_body, jnp.zeros_like(xt), (w13, w2, comb.T))
        y = y + _silu_and_mul(xt @ w13_s.T) @ w2_s.T
        return y.astype(x.dtype).reshape(B, S, D)
    x = x + _L0_xattn_ref(_layernorm(x, axis=-1), ctx_1024, L0_xattn_Wq, L0_xattn_bq, L0_xattn_Wk, L0_xattn_bk, L0_xattn_Wv, L0_xattn_bv, L0_xattn_Wo, L0_xattn_bo)
    x = x + _L0_ffn_ref(_layernorm(x, axis=-1), L0_ffn_W_exp, L0_ffn_b_exp, L0_ffn_up_weights, L0_ffn_up_bias, L0_ffn_down_weights, L0_ffn_W_con, L0_ffn_b_con, L0_ffn_down_bias)
    x = x + _L1_xattn_ref(_layernorm(x, axis=-1), ctx_1024, ctx_1024, L1_xattn_Wq, L1_xattn_bq, L1_xattn_Wk, L1_xattn_bk, L1_xattn_Wv, L1_xattn_bv, L1_xattn_Wo, L1_xattn_bo)
    x = x + _L1_ffn_ref(_layernorm(x, axis=-1), L1_ffn_input_ids, L1_ffn_gate_w, L1_ffn_gate_b, L1_ffn_w13, L1_ffn_w2, L1_ffn_w13_s, L1_ffn_w2_s)
    return x

_drawn_inputs = setup_inputs


def setup_inputs(seed=0):
    import zlib

    import numpy as np

    out = dict(_drawn_inputs(seed))
    spreads = {'L0_xattn_bq': (0.0, 0.8),
     'L0_xattn_bk': (0.0, 0.8),
     'L0_xattn_bv': (0.0, 0.394),
     'L0_xattn_bo': (0.0, 0.1),
     'L0_ffn_b_exp': (0.0, 0.1),
     'L0_ffn_up_bias': (0.0, 0.1),
     'L0_ffn_b_con': (0.0, 0.1),
     'L0_ffn_down_bias': (0.0, 0.1),
     'L1_xattn_bq': (0.0, 0.405),
     'L1_xattn_bk': (0.0, 0.8),
     'L1_xattn_bv': (0.0, 0.1),
     'L1_xattn_bo': (0.0, 0.1)}
    factors = {'L0_xattn_Wq': 8.0,
     'L0_xattn_Wk': 8.0,
     'L1_ffn_gate_w': 8.0,
     'L1_ffn_gate_b': 8.0,
     'L1_ffn_w13': 8.0,
     'L1_ffn_w2': 8.0,
     'L1_ffn_w13_s': 8.0,
     'L1_ffn_w2_s': 8.0}
    for name, (base, spread) in spreads.items():
        noise = np.random.default_rng([zlib.crc32(name.encode()), seed]).standard_normal(out[name].shape)
        drawn = base * np.exp(spread * noise) if base else spread * noise
        out[name] = jnp.asarray(drawn.astype(out[name].dtype))
    for name, factor in factors.items():
        out[name] = (out[name] * factor).astype(out[name].dtype)
    return out
```

```python
import concourse.bass as bass
from concourse import mybir
from contextlib import ExitStack

BATCH, SEQ, D = 4, 256, 128
TOK = BATCH * SEQ
HEADS, DH = 16, 8
PAIRS = HEADS // 2
CH = 512
NCH = TOK // CH
LAYERS = 2
UPL = 2 * BATCH
TERMS_Q = (0, 0, 0, 1, 1, 2)
TERMS_K = (0, 1, 2, 0, 1, 0)
SHIFT = DH * len(TERMS_Q)
HID = 512
BLK = HID // D
EDGE = 254
INTER = 64
EXPERTS = 16
EPAIRS = EXPERTS // 2
TOPK = 4
ROUTE_SCALE = 2.5
EPS = 1e-5
SCALE = DH ** -0.5
EXP_LN = "natural_log_exp_and_others"
GELU = "gelu_and_others"
SILU = "silu_and_others"
BQ, BK, BO, BCON, BDOWN, BUP = 0, 2, 4, 6, 7, 8


def build_program(nc, xT, ctxT, wqkv, woq, cols, mix, bv, gate_b, wexp, wcon, eup, edn, gu, gus, w2p, w2s,
                  gwT, consts, sel, fixed, outT):
    f32, bf16, u16, u32 = mybir.dt.float32, mybir.dt.bfloat16, mybir.dt.uint16, mybir.dt.uint32
    ACT, ALU, AX = mybir.ActivationFunctionType, mybir.AluOpType, mybir.AxisListType
    bounce = nc.dram_tensor("bounce", [4 * LAYERS, len(TERMS_Q), D, CH], bf16).ap()
    shifts = nc.dram_tensor("shifts", [LAYERS * UPL, 8, 2, SEQ], bf16).ap()

    with ExitStack() as ctx:
        def sb(name, shape, dt=f32):
            return ctx.enter_context(nc.sbuf_tensor(name, shape, dt))

        def pb(name, shape):
            return ctx.enter_context(nc.psum_tensor(name, shape, f32))

        def sem(name):
            return ctx.enter_context(nc.semaphore(name))

        eps = sb("eps", [D, 1])
        x = sb("x", [D, TOK])
        cx = sb("cx", [D, TOK])
        xn = sb("xn", [D, TOK])
        w_qkv = sb("w_qkv", [D, LAYERS, 3, D])
        w_o = sb("w_o", [D, LAYERS, 4, D])
        col = sb("col", [D, 12])
        mixc = sb("mixc", [D, 4, 2, 2, 2])
        bvb = sb("bvb", [D, LAYERS, D])
        gbb = sb("gbb", [D, EXPERTS])
        cst = sb("cst", [D, 3, D])
        selt = sb("selt", [80, EPAIRS, D], bf16)
        K = sb("K", [D, 2, PAIRS, TOK], bf16)
        Q = sb("Q", [D, PAIRS, TOK], bf16)
        V = sb("V", [D, 2 * BATCH, HEADS, 32])
        terms = sb("terms", [D, 2, 3, CH], bf16)
        rest = sb("rest", [D, 2, CH])
        P = sb("P", [D, 4, 2, 2, SEQ])
        attn = sb("attn", [D, 4, TOK])
        nm = sb("nm", [D, 2, 2, 8])
        nmT = sb("nmT", [8, 2, 2, SEQ], bf16)
        o_raw = sb("o_raw", [D, 2, CH])
        sums = sb("sums", [D, 2, CH])
        rinv = sums
        sq = sb("sq", [D, 2, CH])
        rstd = sb("rstd", [D, 2, CH])
        w_exp = sb("w_exp", [D, BLK, D + 1])
        w_con = sb("w_con", [D, BLK, D])
        e_up = sb("e_up", [D, BLK, EDGE])
        e_dn = sb("e_dn", [D, BLK, EDGE])
        g_up = sb("g_up", [D, BLK, D + 1])
        mix_a = sb("mix_a", [D, BLK, D + 1])
        mix_b = sb("mix_b", [D, BLK, D + 1])
        w_up = sb("w_up", [D, BLK, D])
        w_dn = sb("w_dn", [D, BLK, D])
        b_up = sb("b_up", [D, BLK])
        b_dn = sb("b_dn", [D, 1])
        w_gu = sb("w_gu", [D, EPAIRS, 2, D])
        w_2 = sb("w_2", [D, EPAIRS, D])
        w_gus = sb("w_gus", [D, 2, INTER])
        w_2s = sb("w_2s", [INTER, D])
        w_g = sb("w_g", [D, EXPERTS])
        route = sb("route", [D, 8, 4, EXPERTS])
        top = sb("top", [D, 4, 8])
        rsum = sb("rsum", [D, 2, 4])
        crest = sb("crest", [EXPERTS, CH])
        cterm = sb("cterm", [EXPERTS, 2, CH], bf16)
        combT = sb("combT", [80, 2, CH], bf16)
        gate_t = sb("gate_t", [D, 2, CH])
        prod_t = sb("prod_t", [D, 2, CH])
        hid_t = sb("hid_t", [D, 2, CH])

        SB = pb("SB", [D, 2, 2, CH])
        MB = pb("MB", [D, 2, CH])
        OB = pb("OB", [D, CH])
        GB = pb("GB", [D, CH])

        x_in = [sem(f"x_in{c}") for c in range(NCH)]
        cx_in = [sem(f"cx_in{c}") for c in range(NCH)]
        cst_in, wqkv_in, col_in, bv_in = sem("cst_in"), sem("wqkv_in"), sem("col_in"), sem("bv_in")
        ffn_in, wo_in, moe_in, fixed_in = sem("ffn_in"), sem("wo_in"), sem("moe_in"), sem("fixed_in")
        eps_set, k_zero0, k_zero1, v_ones, comb_zero = (sem(n) for n in (
            "eps_set", "k_zero0", "k_zero1", "v_ones", "comb_zero"))
        gb_made, gb_read = sem("gb_made"), sem("gb_read")
        squared, rstd_done, xn_done = sem("squared"), sem("rstd_done"), sem("xn_done")
        k_projected, k_read, split_done, bounced = (sem(n) for n in (
            "k_projected", "k_read", "split_done", "bounced"))
        stacked = [sem(f"stacked{m}") for m in range(4 * LAYERS)]
        v_mm, v_done = sem("v_mm"), sem("v_done")
        max_mm, max_red, shift_out = sem("max_mm"), sem("max_red"), sem("shift_out")
        shift_in = [sem(f"shift_in{i}") for i in range(2)]
        scored, exp_done, pv_done, spread, o_copied, o_logged, o_rinv, attn_done = (sem(n) for n in (
            "scored", "exp_done", "pv_done", "spread", "o_copied", "o_logged", "o_rinv", "attn_done"))
        fw_pool, b_built = sem("fw_pool"), sem("b_built")
        up_mm, gelu_done = sem("up_mm"), sem("gelu_done")
        comb_done, combT_done = sem("comb_done"), sem("combT_done")
        gate_mm, silu_done, prod_done, hid_done = sem("gate_mm"), sem("silu_done"), sem("prod_done"), sem("hid_done")
        hid_used, moe_added = sem("hid_used"), sem("moe_added")
        dve_self, pool_self = sem("dve_self"), sem("pool_self")
        stored = sem("stored")

        def chunk(c):
            return slice(c * CH, (c + 1) * CH)

        PROJ = [(0, 1, 0), (0, 0, 0), (0, 1, 1), (0, 0, 1), (1, 1, 0), (1, 0, 0), (1, 1, 1), (1, 0, 1)]
        NORM = [(0, 0), (0, 1), (1, 0), (2, 0), (1, 1), (2, 1), (3, 0), (3, 1)]

        def unit(U):
            l, u = divmod(U, UPL)
            return l, u // 2, u % 2

        def queries(b):
            return slice(b * SEQ, (b + 1) * SEQ)

        UNITS = LAYERS * UPL
        PLAN = {(U, k): [] for U in range(UNITS + 1) for k in range(-1, 4)}

        def maxima_at(U, *points):
            n = 8 // len(points)
            for at, point in enumerate(points):
                PLAN[point] += [("maximum", U, i) for i in range(at * n, (at + 1) * n)]

        def quarters(U):
            return [(U, k) for k in range(4)]

        maxima_at(0, (0, -1))
        PLAN[0, -1] += [("turn", 0)]
        maxima_at(1, (0, -1))
        PLAN[8, -1] += [("turn", 8)]
        for U in range(UNITS + 1):
            if U:
                PLAN[(U, -1) if U in (8, UNITS) else (U, 1)] += [("weighted", U - 1, 1)]
            if U < UNITS:
                if U + 1 < UNITS and U + 1 != 8:
                    PLAN[U, 0] += [("turn", U + 1)]
                PLAN[U, 3] += [("weighted", U, 0)]
        maxima_at(9, (8, -1))
        for U in range(UNITS):
            if U not in (0, 1, 8, 9):
                maxima_at(U, *quarters(U - 2))
        maxima_at(8, *quarters(7))
        for point, steps in {
            (1, 3): [("fw", 0)], (2, 1): [("fw", 1)], (2, 3): [("fw", 2)], (3, 3): [("fw", 3)],
            (4, 0): [("project", 4)], (4, 2): [("values", 0)], (4, 3): [("out", 0, 0)],
            (5, 0): [("centre", 2)], (5, 1): [("average", 2)], (5, 2): [("up", 0)], (5, 3): [("down", 0)],
            (6, 0): [("centre", 3)], (6, 1): [("average", 3)], (6, 2): [("project", 5)],
            (8, -1): [("project", 6), ("out", 0, 1)], (8, 0): [("centre", 4)], (8, 1): [("average", 4)],
            (8, 2): [("up", 1)], (8, 3): [("down", 1)],
            (9, 0): [("centre", 5)], (9, 1): [("average", 5)], (9, 2): [("project", 7)], (9, 3): [("values", 1)],
            (12, 3): [("out", 1, 0)], (13, 0): [("centre", 6)], (13, 1): [("average", 6)],
            (13, 2): [("logits", 0)], (14, 2): [("comb", 0)],
        }.items():
            PLAN[point] += steps

        def up_at(c):
            return next(point[0] for point, steps in PLAN.items() if ("up", c) in steps)

        def do_plan(engine_steps, pair=None):
            for (U, k), steps in PLAN.items():
                if pair and U < UNITS and k >= 0:
                    pair(U, k)
                for step, *args in steps:
                    if step in engine_steps:
                        engine_steps[step](*args)

        gb_no = {}

        block = ctx.enter_context(nc.Block())

        @block.tensor
        def _(pe):
            CENTRE, MEAN, EYE = (cst[:, i, :] for i in range(3))

            def mm(out, lhsT, rhs, start=True, stop=True):
                return nc.tensor.matmul(out, lhsT, rhs, start=start, stop=stop)

            def take_gb(*step):
                if gb_no:
                    pe.wait_ge(gb_read, len(gb_no))
                gb_no[step] = len(gb_no) + 1

            def centre(n):
                s, c = NORM[n]
                take_gb("centre", n)
                if s == 0:
                    pe.wait_ge(x_in[c], 16)
                    pe.wait_ge(cst_in, 16)
                mm(GB[:, :], CENTRE, x[:, chunk(c)]).then_inc(gb_made, 1)

            def average(n):
                s, c = NORM[n]
                take_gb("average", n)
                pe.wait_ge(squared, n + 1)
                mm(GB[:, :], MEAN, sq[:, c, :]).then_inc(gb_made, 1)

            def project_first_keys(c):
                if c == 0:
                    pe.wait_ge(wqkv_in, 16)
                else:
                    pe.wait_ge(k_read, 1)
                pe.wait_ge(cx_in[c], 16)
                mm(OB[:, :], w_qkv[:, 0, 1, :], cx[:, chunk(c)]).then_inc(k_projected, 1)

            def project(m):
                l, is_k, c = PROJ[m]
                take_gb("project", m)
                if not is_k:
                    pe.wait_ge(xn_done, NORM.index((2 * l, c)) + 1)
                src = cx if is_k else xn
                mm(GB[:, :], w_qkv[:, l, is_k, :], src[:, chunk(c)]).then_inc(gb_made, 1)

            def value_products(bank, l, c):
                for t in range(4):
                    at = c * CH + t * D
                    last = mm(bank[:, D * t:D * t + D], cx[:, at:at + D], w_qkv[:, l, 2, :])
                return last

            def next_values(c):
                take_gb("values", c)
                value_products(GB, 1, c).then_inc(gb_made, 1)

            def maxima(U, i):
                l, b, g = unit(U)
                k, qt = divmod(i, 2)
                p = 4 * g + k
                if i == 0 and U % 4 == 0:
                    c = b // 2
                    pe.wait_ge(stacked[PROJ.index((l, 1, c))], 2 * 16)
                    pe.wait_ge(stacked[PROJ.index((l, 0, c))], (2 + 2 * l) * 16)
                    if U == 0:
                        pe.wait_ge(fixed_in, 4 * 16)
                        pe.wait_ge(k_zero0, 2)
                    if U == 4:
                        pe.wait_ge(k_zero1, 2)
                if 8 * U + i >= 2:
                    pe.wait_ge(max_red, 8 * U + i - 1)
                elif i == 0:
                    pe.wait_ge(v_done, 2)
                q0 = b * SEQ + qt * D
                mm(MB[:, i % 2, :].rearrange("p (h s) -> p h s", h=2), Q[:, p, q0:q0 + D],
                   K[:, :, p, queries(b)]).then_inc(max_mm, 1)

            def turn(U):
                take_gb("turn", U)
                pe.wait_ge(max_red, 8 * (U + 1))
                for qt in range(2):
                    last = mm(GB[0:8, D * qt:D * qt + D], nm[:, U % 2, qt, :], EYE)
                last.then_inc(gb_made, 1)

            def scores(U, k):
                l, b, g = unit(U)
                i = 4 * U + k
                if k == 0:
                    pe.wait_ge(shift_in[U % 2], 32 * (U // 2 + 1))
                if i >= 2:
                    pe.wait_ge(exp_done, i - 1)
                for kt in range(2):
                    s0 = b * SEQ + kt * D
                    for hh in range(2):
                        last = mm(SB[:, i % 2, kt, hh * SEQ:(hh + 1) * SEQ], K[:, hh, 4 * g + k, s0:s0 + D],
                                  Q[:, 4 * g + k, queries(b)])
                last.then_inc(scored, 1)

            ups = []

            def weighted(U, half):
                l, b, g = unit(U)
                pe.wait_ge(exp_done, 4 * U + 2 * half + 2)
                if half == 0 and U:
                    pe.wait_ge(o_copied, U)
                    if ups:
                        pe.wait_ge(gelu_done, 3 * len(ups))
                for kt in range(2):
                    for j in range(4):
                        k, hh = 2 * half + j // 2, j % 2
                        h = 2 * (4 * g + k) + hh
                        last = mm(OB[32 * j:32 * j + 32, half * SEQ:(half + 1) * SEQ], V[:, 2 * b + kt, h, :],
                                  P[:, (4 * U + k) % 4, kt, hh, :], start=kt == 0, stop=kt == 1)
                last.then_inc(pv_done, 1)

            def out_project(l, c):
                take_gb("out", l, c)
                pe.wait_ge(attn_done, UPL * l + 4 * c + 4)
                if l == 0 and c == 0:
                    pe.wait_ge(wo_in, 16)
                for i in range(4):
                    last = mm(GB[:, :], w_o[:, l, i, :], attn[:, i, chunk(c)], start=i == 0, stop=i == 3)
                last.then_inc(gb_made, 1)

            def fw(step):
                take_gb("fw", step)
                if step == 0:
                    pe.wait_ge(fw_pool, 1)
                    for b in range(BLK):
                        last = mm(GB[:, D * b:D * b + D], e_up[:, b, EDGE - D:EDGE], w_exp[:, b, 0:D])
                elif step == 1:
                    for b in range(BLK):
                        last = mm(GB[:, b:b + 1], e_up[:, b, EDGE - D:EDGE], w_exp[:, b, D:D + 1])
                elif step == 2:
                    pe.wait_ge(fw_pool, 2)
                    for b in range(BLK):
                        last = mm(GB[:, D * b:D * b + D], e_dn[:, b, EDGE - D:EDGE], w_con[:, b, :])
                else:
                    pe.wait_ge(fw_pool, 3)
                    for b in range(BLK):
                        last = mm(GB[:, D * b:D * b + D], g_up[:, b, 0:D], EYE)
                last.then_inc(gb_made, 1)

            def up(c):
                take_gb("up", c)
                pe.wait_ge(xn_done, NORM.index((1, c)) + 1)
                pe.wait_ge(o_copied, up_at(c))
                for k in range(BLK):
                    if k >= 2:
                        pe.wait_ge(gelu_done, 3 * c + k - 1)
                    mm((OB, GB)[k % 2][:, :], w_up[:, k, :], xn[:, chunk(c)])\
                        .then_inc(up_mm if k < BLK - 1 else gb_made, 1)
                ups.append(c)

            def down(c):
                take_gb("down", c)
                pe.wait_ge(gelu_done, 3 * c + 3)
                for k in range(BLK):
                    last = mm(GB[:, :], w_dn[:, k, :], attn[:, k, chunk(c)], start=k == 0, stop=k == BLK - 1)
                last.then_inc(gb_made, 1)

            def router_logits(c):
                take_gb("logits", c)
                pe.wait_ge(moe_in, 7 * 16)
                pe.wait_ge(xn_done, NORM.index((3, c)) + 1)
                for t in range(4):
                    at = c * CH + t * D
                    last = mm(GB[:, 16 * t:16 * t + 16], xn[:, at:at + D], w_g[:, :])
                last.then_inc(gb_made, 1)

            def turn_weights(c):
                take_gb("comb", c)
                pe.wait_ge(comb_done, c + 1)
                for t in range(4):
                    last = mm(GB[0:16, D * t:D * t + D], route[:, 6 + c, t, :], EYE)
                last.then_inc(gb_made, 1)

            steps = {"centre": centre, "average": average, "project": project, "values": next_values,
                     "out": out_project, "fw": fw, "up": up, "down": down, "logits": router_logits,
                     "comb": turn_weights, "maximum": maxima, "turn": turn, "weighted": weighted}

            centre(0)
            project_first_keys(0)
            average(0)
            centre(1)
            project(1)
            average(1)
            project_first_keys(1)
            project(3)
            for c in range(NCH):
                value_products(MB[:, c, :], 0, c).then_inc(v_mm, 1)
            pe.wait_ge(k_read, 2)
            do_plan(steps, scores)

            beside = {0: (out_project, 1, 1), 1: (centre, 7), 2: (average, 7), 3: (router_logits, 1), 6: (turn_weights, 1)}
            pe.wait_ge(exp_done, 4 * UPL * LAYERS)
            pe.wait_ge(max_red, 8 * UPL * LAYERS)

            for c in range(NCH):
                pe.wait_ge(combT_done, 2 * (c + 1))

                def down_product(e):
                    i = (EPAIRS + 1) * c + e
                    rows = D if e < EPAIRS else INTER
                    if i == 0:
                        pe.wait_ge(o_copied, UPL * LAYERS)
                    if e == 0 and c:
                        pe.wait_ge(moe_added, c)
                    if e < EPAIRS:
                        pe.wait_ge(hid_done, EPAIRS * c + e + 1)
                    else:
                        pe.wait_ge(prod_done, i + 1)
                    w = w_2[:, e, :] if e < EPAIRS else w_2s[:, :]
                    mm(OB[:, :], w, hid_t[0:rows, i % 2, :], start=e == 0, stop=e == EPAIRS).then_inc(hid_used, 1)

                for e in range(EPAIRS + 1):
                    i = (EPAIRS + 1) * c + e
                    rows = D if e < EPAIRS else INTER
                    if i >= 2:
                        pe.wait_ge(prod_done, i - 1)
                        pe.wait_ge(hid_done, EPAIRS * c + e - 1 if e else EPAIRS * c)
                    for j in range(2):
                        w = w_gu[:, e, j, :] if e < EPAIRS else w_gus[:, j, :]
                        last = mm(SB[0:rows, i % 2, j, :], w, xn[:, chunk(c)])
                    if e < EPAIRS:
                        last = mm(MB[:, i % 2, :], selt[:, e, :], combT[:, c, :])
                    last.then_inc(gate_mm, 1)
                    if c == 0 and e in beside:
                        step, *args = beside[e]
                        step(*args)
                    if e:
                        down_product(e - 1)
                down_product(EPAIRS)

        @block.sync
        def _(sp):
            def stack(m):
                l, is_k, c = PROJ[m]
                sp.wait_ge(split_done, m + 1)
                t = terms[:, m % 2, :, :]
                if is_k:
                    parts = ((0, 3, t), (3, 5, t[:, 0:2, :]), (5, 6, t[:, 0:1, :]))
                else:
                    parts = ((0, 3, t[:, 0:1, :].broadcast_to([D, 3, CH])),
                             (3, 5, t[:, 1:2, :].broadcast_to([D, 2, CH])), (5, 6, t[:, 2:3, :]))
                for t0, t1, src in parts:
                    sp.dma_start(bounce[m, t0:t1, :, :].rearrange("t r n -> r t n"), src).then_inc(bounced, 16)
                sp.wait_ge(bounced, 48 * (m + 1))
                if l:
                    sp.wait_ge(scored, 4 * 4 * (c + 1))
                for hh in range(2):
                    dst = K[64 * hh:64 * hh + SHIFT, hh, :, chunk(c)] if is_k \
                        else Q[64 * hh:64 * hh + SHIFT, :, chunk(c)]
                    src = bounce[m, :, 64 * hh:64 * hh + 64, :].rearrange("t (d p) n -> t d p n", d=DH)
                    sp.dma_start(dst, src).then_inc(stacked[m], 16)
                if l and not is_k:
                    for hh in range(2):
                        sp.dma_start(Q[64 * hh + SHIFT:64 * hh + SHIFT + 2, :, chunk(c)].bitcast(u16),
                                     fixed[1, 0:PAIRS * CH].rearrange("(p n) -> p n", p=PAIRS)
                                     .partition_broadcast(2)).then_inc(stacked[m], 16)

            def shift_rows(U):
                l, b, g = unit(U)
                sp.wait_ge(gb_read, gb_no["turn", U])
                sp.dma_start(shifts[U], nmT[:, U % 2, :, :]).then_inc(shift_out, 16)
                sp.wait_ge(shift_out, 16 * (U + 1))
                for hh in range(2):
                    sp.dma_start(Q[64 * hh + SHIFT:64 * hh + SHIFT + 2, 4 * g:4 * g + 4, queries(b)],
                                 shifts[U, 4 * hh:4 * hh + 4, :, :].rearrange("k i q -> i k q"))\
                        .then_inc(shift_in[U % 2], 16)

            sp.dma_start(x[:, chunk(0)], xT[:, chunk(0)]).then_inc(x_in[0], 16)
            sp.dma_start(cx[:, chunk(0)], ctxT[:, chunk(0)]).then_inc(cx_in[0], 16)
            sp.dma_start(x[:, chunk(1)], xT[:, chunk(1)]).then_inc(x_in[1], 16)
            sp.dma_start(cx[:, chunk(1)], ctxT[:, chunk(1)]).then_inc(cx_in[1], 16)
            for hh in range(2):
                sp.dma_start(K[64 * hh + SHIFT:64 * hh + 64, hh, :, :].bitcast(u16),
                             fixed[0].rearrange("(p n) -> p n", p=PAIRS).partition_broadcast(64 - SHIFT))\
                    .then_inc(fixed_in, 16)
                sp.dma_start(Q[64 * hh + SHIFT:64 * hh + 64, :, :].bitcast(u16),
                             fixed[1].rearrange("(p n) -> p n", p=PAIRS).partition_broadcast(64 - SHIFT))\
                    .then_inc(fixed_in, 16)
            sp.dma_start(bvb[:, :, :], bv.rearrange("l d -> (l d)").partition_broadcast(D)).then_inc(bv_in, 16)
            for m in range(4):
                stack(m)
            do_plan({"project": stack, "turn": shift_rows})
            for c in range(NCH):
                sp.wait_ge(moe_added, c + 1)
                sp.dma_start(outT[:, chunk(c)], x[:, chunk(c)]).then_inc(stored, 16)
            sp.wait_ge(stored, 16 * NCH)

        @block.gpsimd
        def _(pool):
            steps = [0]

            def link(ins):
                steps[0] += 1
                ins.then_inc(pool_self, 1)
                pool.wait_ge(pool_self, steps[0])

            for c in range(NCH):
                pool.wait_ge(x_in[c], 16)
                pool.wait_ge(cx_in[c], 16)
            for dst, src in ((e_up[:, :, :], eup), (e_dn[:, :, :], edn), (mixc[:, :, :, :, :], mix),
                             (w_exp[:, :, :], wexp), (w_con[:, :, :], wcon)):
                pool.dma_start(dst, src).then_inc(ffn_in, 16)
            pool.dma_start(w_o[:, :, :, :], woq).then_inc(wo_in, 16)
            for hh in range(2):
                nc.gpsimd.memset(K[64 - 64 * hh:128 - 64 * hh, hh, :, chunk(1)].bitcast(u32), 0).then_inc(k_zero1, 1)
                pool.wait_ge(k_zero1, hh + 1)
            nc.gpsimd.memset(V[:, :, :, DH:32], 1.0).then_inc(v_ones, 1)
            pool.wait_ge(v_ones, 1)
            nc.gpsimd.memset(combT[:, :, :].bitcast(u32), 0).then_inc(comb_zero, 1)
            pool.wait_ge(comb_zero, 1)

            pool.wait_ge(ffn_in, 5 * 16)
            for s in range(1, 7):
                w = 2 ** s
                at = 2 * w - 2
                old = e_up[:, :, at - w:at].unsqueeze(2).broadcast_to([D, BLK, 2, w])
                new = e_up[:, :, at:at + 2 * w].rearrange("p b (o i) -> p b o i", o=2)
                link(nc.gpsimd.tensor_tensor(new, new, old, ALU.mult))
            for s in range(1, 7):
                w = 2 ** s
                at = 2 * w - 2
                old = e_dn[:, :, at - w:at].unsqueeze(3).broadcast_to([D, BLK, w, 2])
                new = e_dn[:, :, at:at + 2 * w].rearrange("p b (i o) -> p b i o", o=2)
                ins = nc.gpsimd.tensor_tensor(new, new, old, ALU.mult)
                if s < 6:
                    link(ins)
            ins.then_inc(fw_pool, 1)

            def mix_blocks(k, low, dst, src, n):
                s4 = src.rearrange("p (h l) n -> p h l n", h=2)
                d4 = dst.rearrange("p (h l) n -> p h l n", h=2)
                for i, t in ((0, mix_a), (1, mix_b)):
                    s = s4[:, :, i:i + 1, :] if low else s4[:, i:i + 1, :, :]
                    t4 = t[:, :, 0:n].rearrange("p (h l) n -> p h l n", h=2)
                    cc = mixc[:, k, :, :, i:i + 1].broadcast_to([D, 2, 2, n])
                    ins = nc.gpsimd.tensor_tensor(t4, s.broadcast_to([D, 2, 2, n]), cc, ALU.mult)
                    link(ins)
                return nc.gpsimd.tensor_tensor(d4, mix_a[:, :, 0:n].rearrange("p (h l) n -> p h l n", h=2),
                                               mix_b[:, :, 0:n].rearrange("p (h l) n -> p h l n", h=2), ALU.add)

            link(mix_blocks(2, False, w_con[:, :, :], w_con[:, :, :], D))
            mix_blocks(3, True, w_con[:, :, :], w_con[:, :, :], D).then_inc(fw_pool, 1)

            def normalise(U):
                l, b, g = unit(U)
                pool.wait_ge(o_rinv, U + 1)
                if l and U % 4 == 0:
                    pool.wait_ge(gb_read, gb_no["down", b // 2])
                nc.gpsimd.tensor_tensor(attn[:, 2 * g:2 * g + 2, queries(b)],
                                        o_raw[:, U % 2, :].rearrange("p (h q) -> p h q", h=2),
                                        rinv[:, U % 2, :].rearrange("p (h q) -> p h q", h=2),
                                        ALU.mult).then_inc(attn_done, 1)

            def load_experts():
                for dst, src in ((w_gu[:, :, :, :], gu), (w_2[:, :, :], w2p), (w_gus[:, :, :], gus), (w_2s[:, :], w2s),
                                 (w_g[:, :], gwT), (selt[:, :, :].bitcast(u16), sel),
                                 (gbb[:, :], gate_b.partition_broadcast(D))):
                    pool.dma_start(dst, src).then_inc(moe_in, 16)

            def mix_up():
                pool.wait_ge(gb_read, gb_no["fw", 1])
                pool.wait_ge(fw_pool, 2)
                link(mix_blocks(0, True, g_up[:, :, :], g_up[:, :, :], D + 1))
                mix_blocks(1, False, g_up[:, :, :], g_up[:, :, :], D + 1).then_inc(fw_pool, 1)

            def after_weighted(U, half):
                if half:
                    normalise(U)
                    if U == 1:
                        mix_up()
                        load_experts()

            do_plan({"weighted": after_weighted})

        @block.scalar
        def _(act):
            act.dma_start(cst[:, :, :], consts).then_inc(cst_in, 16)
            act.dma_start(w_qkv[:, :, :, :], wqkv).then_inc(wqkv_in, 16)
            act.dma_start(col[:, :], cols).then_inc(col_in, 16)

            def square(n):
                c = NORM[n][1]
                act.wait_ge(gb_read, gb_no["centre", n])
                nc.scalar.activation(sq[:, c, :], xn[:, chunk(c)], ACT.Square).then_inc(squared, 1)

            def rstd_of(n):
                c = NORM[n][1]
                act.wait_ge(gb_made, gb_no["average", n])
                nc.scalar.activation(rstd[:, c, :], GB[:, :], ACT.Ln, bias=eps[:, 0:1]).then_inc(gb_read, 1)
                act.wait_ge(gb_read, gb_no["average", n])
                nc.scalar.activation(rstd[:, c, :], rstd[:, c, :], ACT.Exp, scale=-0.5).then_inc(rstd_done, 1)

            def exps(U, k):
                i = 4 * U + k
                act.wait_ge(scored, i + 1)
                if i >= 4:
                    act.wait_ge(pv_done, (i - 4) // 2 + 1)
                nc.scalar.activation(P[:, i % 4, :, :, :].rearrange("p k h q -> p (k h q)"),
                                     SB[:, i % 2, :, :].rearrange("p k n -> p (k n)"),
                                     ACT.Exp, scale=SCALE).then_inc(exp_done, 1)

            def invert(U):
                act.wait_ge(spread, U + 1)
                if U >= 2:
                    act.wait_ge(attn_done, U - 1)
                nc.scalar.activation(o_raw[:, U % 2, :], OB[:, :], ACT.Copy).then_inc(o_copied, 1)
                nc.scalar.activation(rinv[:, U % 2, :], sums[:, U % 2, :], ACT.Ln).then_inc(o_logged, 1)
                act.wait_ge(o_logged, U + 1)
                nc.scalar.activation(rinv[:, U % 2, :], rinv[:, U % 2, :], ACT.Exp, scale=-1.0).then_inc(o_rinv, 1)

            def gelu(c):
                act.preload_act_table_set(GELU)
                for k in range(BLK):
                    if k < BLK - 1:
                        act.wait_ge(up_mm, 3 * c + k + 1)
                    else:
                        act.wait_ge(gb_made, gb_no["up", c])
                    nc.scalar.activation(attn[:, k, chunk(c)], (OB, GB)[k % 2][:, :], ACT.Gelu,
                                         bias=b_up[:, k:k + 1]).then_inc(gelu_done if k < BLK - 1 else gb_read, 1)
                act.preload_act_table_set(EXP_LN)

            def router_exp(c):
                act.wait_ge(gb_made, gb_no["logits", c])
                nc.scalar.activation(route[:, c, :, :], GB[:, 0:64].rearrange("p (t e) -> p t e", e=EXPERTS),
                                     ACT.Exp, scale=-1.0).then_inc(gb_read, 1)

            def after_weighted(U, half):
                if half:
                    invert(U)

            steps = {"centre": square, "average": rstd_of, "up": gelu, "logits": router_exp,
                     "weighted": after_weighted}

            act.preload_act_table_set(EXP_LN)
            act.wait_ge(eps_set, 1)
            square(0)
            rstd_of(0)
            square(1)
            rstd_of(1)
            do_plan(steps, exps)
            beside = {1: (square, 7), 2: (rstd_of, 7), 3: (router_exp, 1)}
            for c in range(NCH):
                for e in range(EPAIRS + 1):
                    i = (EPAIRS + 1) * c + e
                    rows = D if e < EPAIRS else INTER
                    if i == 0:
                        act.preload_act_table_set(SILU)
                    act.wait_ge(gate_mm, i + 1)
                    if i >= 2:
                        act.wait_ge(prod_done, i - 1)
                    nc.scalar.activation(gate_t[0:rows, i % 2, :], SB[0:rows, i % 2, 0, :], ACT.Silu).then_inc(silu_done, 1)
                    if c == 0 and e in beside:
                        step, *args = beside[e]
                        if step == rstd_of:
                            act.preload_act_table_set(EXP_LN)
                        step(*args)
                        if step == router_exp:
                            act.preload_act_table_set(SILU)

        @block.vector
        def _(dve):
            links = [0]

            def link(ins):
                links[0] += 1
                ins.then_inc(dve_self, 1)
                dve.wait_ge(dve_self, links[0])

            def split(m):
                l, is_k, c = PROJ[m]
                bank = OB if (l, is_k) == (0, 1) else GB
                bias = col[:, (BK if is_k else BQ) + l:(BK if is_k else BQ) + l + 1]
                t = terms[:, m % 2, :, :]
                r = rest[:, m % 2, :]
                if bank is OB:
                    dve.wait_ge(k_projected, c + 1)
                else:
                    dve.wait_ge(gb_made, gb_no["project", m])
                if m == 0:
                    dve.wait_ge(col_in, 16)
                if m >= 2:
                    dve.wait_ge(bounced, 48 * (m - 1))
                link(nc.vector.tensor_scalar(t[:, 0, :], bank[:, :], bias, None, ALU.add))
                read = nc.vector.scalar_tensor_tensor(r, bank[:, :], bias, t[:, 0, :], ALU.add, ALU.subtract)
                if bank is OB:
                    read.then_inc(k_read, 1)
                    dve.wait_ge(k_read, c + 1)
                else:
                    read.then_inc(gb_read, 1)
                    dve.wait_ge(gb_read, gb_no["project", m])
                link(nc.vector.tensor_copy(t[:, 1, :], r))
                nc.vector.tensor_tensor(t[:, 2, :], r, t[:, 1, :], ALU.subtract).then_inc(split_done, 1)

            def centred(n):
                c = NORM[n][1]
                dve.wait_ge(gb_made, gb_no["centre", n])
                nc.vector.tensor_copy(xn[:, chunk(c)], GB[:, :]).then_inc(gb_read, 1)

            def normed(n):
                c = NORM[n][1]
                dve.wait_ge(rstd_done, n + 1)
                nc.vector.tensor_tensor(xn[:, chunk(c)], xn[:, chunk(c)], rstd[:, c, :], ALU.mult).then_inc(xn_done, 1)

            def add_value_bias(l, c, bank):
                bias = bvb[:, l, :].rearrange("p (h d) -> p h d", d=DH)
                for t in range(4):
                    last = nc.vector.tensor_tensor(V[:, 4 * c + t, :, 0:DH],
                                                   bank[:, D * t:D * t + D].rearrange("p (h d) -> p h d", d=DH),
                                                   bias, ALU.add)
                return last

            def first_values(c):
                dve.wait_ge(v_mm, c + 1)
                if c == 0:
                    dve.wait_ge(bv_in, 16)
                    dve.wait_ge(v_ones, 1)
                add_value_bias(0, c, MB[:, c, :]).then_inc(v_done, 1)

            def next_values(c):
                dve.wait_ge(gb_made, gb_no["values", c])
                dve.wait_ge(pv_done, 2 * 4 * (c + 1))
                add_value_bias(1, c, GB).then_inc(gb_read, 1)

            def reduce(U, i):
                k, qt = divmod(i, 2)
                dve.wait_ge(max_mm, 8 * U + i + 1)
                nc.vector.tensor_reduce(nm[:, U % 2, qt, k:8:4], MB[:, i % 2, :].rearrange("p (h s) -> p h s", h=2),
                                        AX.X, ALU.max, negate=True).then_inc(max_red, 1)

            def split_max(U):
                dve.wait_ge(gb_made, gb_no["turn", U])
                if U >= 2:
                    dve.wait_ge(shift_out, 16 * (U - 1))
                link(nc.vector.tensor_copy(nmT[:, U % 2, 0, :], GB[0:8, 0:SEQ]))
                nc.vector.tensor_tensor(nmT[:, U % 2, 1, :], GB[0:8, 0:SEQ], nmT[:, U % 2, 0, :],
                                        ALU.subtract).then_inc(gb_read, 1)

            def spread_sums(U):
                dve.wait_ge(pv_done, 2 * (U + 1))
                if U >= 2:
                    dve.wait_ge(attn_done, U - 1)
                nc.vector.stream_shuffle(sums[:, U % 2, :], OB[:, :], [DH] * 32).then_inc(spread, 1)

            def residual(c, bias, *step):
                dve.wait_ge(gb_made, gb_no[step])
                nc.vector.scalar_tensor_tensor(x[:, chunk(c)], GB[:, :], bias, x[:, chunk(c)],
                                               ALU.add, ALU.add).then_inc(gb_read, 1)

            def add_attention(l, c):
                residual(c, col[:, BO + l:BO + l + 1], "out", l, c)

            def add_ffn(c):
                dve.wait_ge(b_built, 1)
                residual(c, b_dn[:, 0:1], "down", c)

            def fw_read(step):
                dve.wait_ge(gb_made, gb_no["fw", step])
                if step == 1:
                    dst, src = g_up[:, :, D:D + 1], GB[:, 0:BLK].unsqueeze(2)
                else:
                    dst = (g_up[:, :, 0:D], None, w_dn[:, :, :], w_up[:, :, :])[step]
                    src = GB[:, :].rearrange("p (b n) -> p b n", b=BLK)
                if step == 3:
                    nc.vector.tensor_tensor(b_dn[:, :], col[:, BCON:BCON + 1], col[:, BDOWN:BDOWN + 1], ALU.add)\
                        .then_inc(b_built, 1)
                    link(nc.vector.tensor_tensor(b_up[:, :], g_up[:, :, D:D + 1].rearrange("p b o -> p (b o)"),
                                                 col[:, BUP:BUP + BLK], ALU.add))
                nc.vector.tensor_copy(dst, src).then_inc(gb_read, 1)

            def routing(c):
                ex, sc, bi, le, ws = (route[:, i, :, :] for i in (c, 2, 3, 4, 5))
                dve.wait_ge(gb_read, gb_no["logits", c])
                link(nc.vector.tensor_scalar(ex, ex, 1.0, None, ALU.add))
                link(nc.vector.reciprocal(sc, ex))
                link(nc.vector.tensor_tensor(bi, sc, gbb[:, :].unsqueeze(1).broadcast_to([D, 4, EXPERTS]), ALU.add))
                for t in range(4):
                    ins = nc.vector.max(top[:, t, :], bi[:, t, :])
                link(ins)
                link(nc.vector.memset(top[:, :, TOPK:8], -3.0e38))
                for t in range(4):
                    ins = nc.vector.match_replace(out=le[:, t, :], in_to_replace=top[:, t, :], in_values=bi[:, t, :],
                                                  imm_value=-1.0e38)
                link(ins)
                link(nc.vector.tensor_tensor(le, le, bi, ALU.not_equal))
                link(nc.vector.tensor_tensor(ws, sc, le, ALU.mult))
                link(nc.vector.reduce_sum(rsum[:, 0, :], ws, AX.X))
                link(nc.vector.reciprocal(rsum[:, 1, :], rsum[:, 0, :]))
                nc.vector.scalar_tensor_tensor(route[:, 6 + c, :, :], ws, ROUTE_SCALE,
                                               rsum[:, 1, :].unsqueeze(2).broadcast_to([D, 4, EXPERTS]),
                                               ALU.mult, ALU.mult).then_inc(comb_done, 1)

            def weight_terms(c):
                dve.wait_ge(gb_made, gb_no["comb", c])
                dve.wait_ge(comb_zero, 1)
                link(nc.vector.tensor_copy(combT[0:16, c, :], GB[0:16, :]))
                if c:
                    dve.wait_ge(combT_done, 2 * c)
                nc.vector.tensor_tensor(crest[:, :], GB[0:16, :], combT[0:16, c, :], ALU.subtract).then_inc(gb_read, 1)
                dve.wait_ge(gb_read, gb_no["comb", c])
                link(nc.vector.tensor_copy(cterm[:, 0, :], crest[:, :]))
                link(nc.vector.tensor_tensor(cterm[:, 1, :], crest[:, :], cterm[:, 0, :], ALU.subtract))
                nc.vector.tensor_copy(combT[32:48, c, :], cterm[:, 0, :]).then_inc(combT_done, 1)
                nc.vector.tensor_copy(combT[64:80, c, :], cterm[:, 1, :]).then_inc(combT_done, 1)

            def after_weighted(U, half):
                if half:
                    spread_sums(U)

            def first_routing(c):
                dve.wait_ge(moe_in, 7 * 16)
                routing(c)

            steps = {"centre": centred, "average": normed, "project": split, "values": next_values,
                     "out": add_attention, "fw": fw_read, "down": add_ffn, "logits": first_routing,
                     "comb": weight_terms, "maximum": reduce, "turn": split_max, "weighted": after_weighted}

            nc.vector.memset(eps[:, :], EPS).then_inc(eps_set, 1)
            for hh in range(2):
                nc.vector.memset(K[64 - 64 * hh:128 - 64 * hh, hh, :, chunk(0)].bitcast(u32), 0).then_inc(k_zero0, 1)
            centred(0)
            split(0)
            normed(0)
            centred(1)
            split(1)
            normed(1)
            split(2)
            split(3)
            for c in range(NCH):
                first_values(c)
            do_plan(steps)
            beside = {0: (add_attention, 1, 1), 1: (centred, 7), 2: (normed, 7), 3: (routing, 1), 6: (weight_terms, 1)}
            for c in range(NCH):
                for e in range(EPAIRS + 1):
                    i = (EPAIRS + 1) * c + e
                    rows = D if e < EPAIRS else INTER
                    dve.wait_ge(silu_done, i + 1)
                    if i >= 2:
                        dve.wait_ge(hid_used, i - 1)
                    dst = prod_t if e < EPAIRS else hid_t
                    nc.vector.tensor_tensor(dst[0:rows, i % 2, :], SB[0:rows, i % 2, 1, :], gate_t[0:rows, i % 2, :],
                                            ALU.mult).then_inc(prod_done, 1)
                    if e < EPAIRS:
                        dve.wait_ge(prod_done, i + 1)
                        nc.vector.tensor_tensor(hid_t[:, i % 2, :], MB[:, i % 2, :], prod_t[:, i % 2, :],
                                                ALU.mult).then_inc(hid_done, 1)
                    if c == 0 and e in beside:
                        step, *args = beside[e]
                        step(*args)
                dve.wait_ge(hid_used, (EPAIRS + 1) * (c + 1))
                nc.vector.tensor_tensor(x[:, chunk(c)], OB[:, :], x[:, chunk(c)], ALU.add).then_inc(moe_added, 1)


_ORDER = ["xT", "ctxT", "wqkv", "woq", "cols", "mix", "bv", "gate_b", "wexp", "wcon", "eup", "edn", "gu", "gus",
          "w2p", "w2s", "gwT", "consts", "sel", "fixed"]


def _layout(inp):
    import numpy as np
    f = {k: np.asarray(v) for k, v in inp.items()}
    out = {}
    out["xT"] = f["x"].reshape(TOK, D).T
    out["ctxT"] = f["ctx_1024"].reshape(TOK, D).T
    perm = np.arange(D).reshape(PAIRS, 2, DH).transpose(1, 2, 0).reshape(-1)
    ws = []
    for l in range(LAYERS):
        q, k, v = (f[f"L{l}_xattn_W{n}"] for n in "qkv")
        if l == 0:
            q, k, v = q.T, k.T, v.T
        ws.append(np.stack([q[:, perm], k[:, perm], v], 1))
    out["wqkv"] = np.stack(ws, 1)
    wo = np.zeros((4, 32, LAYERS, 4, D), np.float32)
    for l in range(LAYERS):
        o = f[f"L{l}_xattn_Wo"]
        o = o.T if l == 0 else o
        wo[:, :DH, l] = o.reshape(4, 4, DH, D).transpose(1, 2, 0, 3)
    out["woq"] = wo.reshape(D, LAYERS, 4, D)
    vec = [f["L0_xattn_bq"][perm], f["L1_xattn_bq"][perm], f["L0_xattn_bk"][perm], f["L1_xattn_bk"][perm],
           f["L0_xattn_bo"], f["L1_xattn_bo"], f["L0_ffn_b_con"], f["L0_ffn_down_bias"]]
    vec += list(f["L0_ffn_up_bias"].reshape(BLK, D))
    out["cols"] = np.stack(vec, 1)
    up, dn = f["L0_ffn_up_weights"], f["L0_ffn_down_weights"]
    up7, dn7 = (w[7].reshape(2, D, 2, 2) for w in (up, dn))
    up8, dn8 = (w[8].reshape(2, D, 2, 2) for w in (up, dn))
    out["mix"] = np.stack([up7.transpose(1, 0, 2, 3), up8.transpose(1, 2, 0, 3),
                           dn8.transpose(1, 3, 0, 2), dn7.transpose(1, 0, 3, 2)], 1)
    out["bv"] = np.stack([f["L0_xattn_bv"], f["L1_xattn_bv"]])
    out["gate_b"] = f["L1_ffn_gate_b"]
    out["wexp"] = np.concatenate([f["L0_ffn_W_exp"].T, f["L0_ffn_b_exp"][:, None]], 1)\
        .reshape(BLK, D, D + 1).transpose(1, 0, 2)
    out["wcon"] = f["L0_ffn_W_con"].reshape(BLK, D, D).transpose(1, 0, 2)
    eu, ed = [], []
    for s in range(7):
        w = up[s].reshape(HID >> (s + 1), 2 ** s, 2, 2)
        w = w.transpose(0, 3, 2, 1).reshape(HID >> (s + 1), 2, 1, 2 ** (s + 1))
        eu.append(np.broadcast_to(w, (HID >> (s + 1), 2, 2 ** s, 2 ** (s + 1))).reshape(BLK, D, -1))
    for s in range(6, -1, -1):
        w = dn[s].reshape(BLK, 2 ** (6 - s), 2 ** s, 2, 2)
        w = w.transpose(3, 2, 0, 1, 4).reshape(1, 2 ** (s + 1), BLK, 2 ** (7 - s))
        ed.append(np.broadcast_to(w, (2 ** (6 - s), 2 ** (s + 1), BLK, 2 ** (7 - s))).reshape(D, BLK, -1))
    out["eup"] = np.concatenate(eu, 2).transpose(1, 0, 2)
    out["edn"] = np.concatenate(ed, 2)
    w13 = f["L1_ffn_w13"].reshape(EPAIRS, 2, 2, INTER, D)
    out["gu"] = w13.transpose(4, 0, 2, 1, 3).reshape(D, EPAIRS, 2, D)
    out["gus"] = f["L1_ffn_w13_s"].reshape(2, INTER, D).transpose(2, 0, 1)
    out["w2p"] = f["L1_ffn_w2"].reshape(EPAIRS, 2, D, INTER).transpose(1, 3, 0, 2).reshape(D, EPAIRS, D)
    out["w2s"] = f["L1_ffn_w2_s"].T
    out["gwT"] = f["L1_ffn_gate_w"].T
    eye = np.eye(D, dtype=np.float32)
    mean = np.full((D, D), 1.0 / D, np.float32)
    out["consts"] = np.stack([eye - mean, mean, eye], 1)
    sel = np.zeros((3, 32, EPAIRS, 2, INTER), np.uint16)
    for e in range(EXPERTS):
        sel[:, e, e // 2, e % 2] = 0x3F80
    out["sel"] = sel.reshape(96, EPAIRS, D)[:80]
    out["fixed"] = np.repeat(np.array([0x3F80, 0], np.uint16), PAIRS * TOK).reshape(2, PAIRS * TOK)
    return {k: np.ascontiguousarray(v) for k, v in out.items()}


def kernel(**inputs):
    import numpy as np
    import concourse.bacc as bacc
    from concourse.bass_utils import run_bass_kernel_spmd

    nc = bacc.Bacc("TRN2", target_bir_lowering=False, num_devices=1)
    arrays = _layout(inputs)
    args = [nc.dram_tensor(n, arrays[n].shape, mybir.dt.from_np(arrays[n].dtype), kind="ExternalInput").ap()
            for n in _ORDER]
    args.append(nc.dram_tensor("outT", (D, TOK), mybir.dt.float32, kind="ExternalOutput").ap())
    build_program(nc, *args)
    r = run_bass_kernel_spmd(nc, [arrays], core_ids=[0])
    return np.ascontiguousarray(np.asarray(r.results[0]["outT"]).T).reshape(BATCH, SEQ, D)
```

```python
import concourse.bass as bass
from concourse import mybir
from contextlib import ExitStack

BATCH, SEQ, D = 4, 256, 128
TOK = BATCH * SEQ
HEADS, DH = 16, 8
PAIRS = HEADS // 2
CH = 512
NCH = TOK // CH
LAYERS = 2
UPL = 2 * BATCH
TERMS_Q = (0, 0, 0, 1, 1, 2)
TERMS_K = (0, 1, 2, 0, 1, 0)
SHIFT = DH * len(TERMS_Q)
HID = 512
BLK = HID // D
EDGE = 254
INTER = 64
EXPERTS = 16
EPAIRS = EXPERTS // 2
TOPK = 4
ROUTE_SCALE = 2.5
EPS = 1e-5
SCALE = DH ** -0.5
EXP_LN = "natural_log_exp_and_others"
GELU = "gelu_and_others"
SILU = "silu_and_others"
BQ, BK, BO, BCON, BDOWN, BUP = 0, 2, 4, 6, 7, 8


def build_program(nc, xT, ctxT, wqkv, woq, cols, mix, bv, gate_b, wexp, wcon, eup, edn, gu, gus, w2p, w2s,
                  gwT, consts, sel, fixed, outT):
    f32, bf16, u16, u32 = mybir.dt.float32, mybir.dt.bfloat16, mybir.dt.uint16, mybir.dt.uint32
    ACT, ALU, AX = mybir.ActivationFunctionType, mybir.AluOpType, mybir.AxisListType
    bounce = nc.dram_tensor("bounce", [4 * LAYERS, len(TERMS_Q), D, CH], bf16).ap()

    with ExitStack() as ctx:
        def sb(name, shape, dt=f32):
            return ctx.enter_context(nc.sbuf_tensor(name, shape, dt))

        def pb(name, shape):
            return ctx.enter_context(nc.psum_tensor(name, shape, f32))

        def sem(name):
            return ctx.enter_context(nc.semaphore(name))

        eps = sb("eps", [D, 1])
        x = sb("x", [D, TOK])
        cx = sb("cx", [D, TOK])
        xn = sb("xn", [D, TOK])
        w_qkv = sb("w_qkv", [D, LAYERS, 3, D])
        w_o = sb("w_o", [D, LAYERS, 4, D])
        col = sb("col", [D, 12])
        mixc = sb("mixc", [D, 4, 2, 2, 2])
        bvb = sb("bvb", [D, LAYERS, D])
        gbb = sb("gbb", [D, EXPERTS])
        cst = sb("cst", [D, 3, D])
        selt = sb("selt", [80, EPAIRS, D], bf16)
        K = sb("K", [D, 2, PAIRS, TOK], bf16)
        Q = sb("Q", [D, PAIRS, TOK], bf16)
        V = sb("V", [D, 2 * BATCH, HEADS, 32])
        terms = sb("terms", [D, 2, 3, CH], bf16)
        rest = sb("rest", [D, 2, CH])
        P = sb("P", [D, 4, 2, 2, SEQ])
        attn = sb("attn", [D, 4, TOK])
        nm = sb("nm", [D, 2, 2, 8])
        nmT = sb("nmT", [8, 2, 2, SEQ], bf16)
        o_raw = sb("o_raw", [D, 2, CH])
        sums = sb("sums", [D, 2, CH])
        rinv = sums
        sq = sb("sq", [D, 2, CH])
        rstd = sb("rstd", [D, 2, CH])
        w_exp = sb("w_exp", [D, BLK, D + 1])
        w_con = sb("w_con", [D, BLK, D])
        e_up = sb("e_up", [D, BLK, EDGE])
        e_dn = sb("e_dn", [D, BLK, EDGE])
        g_up = sb("g_up", [D, BLK, D + 1])
        mix_a = sb("mix_a", [D, BLK, D + 1])
        mix_b = sb("mix_b", [D, BLK, D + 1])
        w_up = sb("w_up", [D, BLK, D])
        w_dn = sb("w_dn", [D, BLK, D])
        b_up = sb("b_up", [D, BLK])
        b_dn = sb("b_dn", [D, 1])
        w_gu = sb("w_gu", [D, EPAIRS, 2, D])
        w_2 = sb("w_2", [D, EPAIRS, D])
        w_gus = sb("w_gus", [D, 2 * INTER])
        w_2s = sb("w_2s", [D, D])
        w_g = sb("w_g", [D, EXPERTS])
        route = sb("route", [D, 8, 4, EXPERTS])
        top = sb("top", [D, 4, 8])
        rsum = sb("rsum", [D, 2, 4])
        crest = sb("crest", [EXPERTS, CH])
        cterm = sb("cterm", [EXPERTS, 2, CH], bf16)
        combT = sb("combT", [80, 2, CH], bf16)
        gate_t = sb("gate_t", [D, 2, CH])
        prod_t = sb("prod_t", [D, 2, CH])
        hid_t = sb("hid_t", [D, 2, CH])

        SB = pb("SB", [D, 2, 2, CH])
        MB = pb("MB", [D, 2, CH])
        OB = pb("OB", [D, CH])
        GB = pb("GB", [D, CH])

        x_in = [sem(f"x_in{c}") for c in range(NCH)]
        cx_in = [sem(f"cx_in{c}") for c in range(NCH)]
        cst_in, wqkv_in, col_in, bv_in = sem("cst_in"), sem("wqkv_in"), sem("col_in"), sem("bv_in")
        ffn_in, wo_in, moe_in, fixed_in = sem("ffn_in"), sem("wo_in"), sem("moe_in"), sem("fixed_in")
        eps_set, k_zero0, k_zero1, v_ones, comb_zero = (sem(n) for n in (
            "eps_set", "k_zero0", "k_zero1", "v_ones", "comb_zero"))
        gb_made, gb_read = sem("gb_made"), sem("gb_read")
        squared, rstd_done, xn_done = sem("squared"), sem("rstd_done"), sem("xn_done")
        k_projected, k_read, split_done = (sem(n) for n in ("k_projected", "k_read", "split_done"))
        bounced = [sem(f"bounced{m}") for m in range(4 * LAYERS)]
        stacked = [sem(f"stacked{m}") for m in range(4 * LAYERS)]
        v_mm, v_done = sem("v_mm"), sem("v_done")
        max_mm, max_red = sem("max_mm"), sem("max_red")
        shift_in = [sem(f"shift_in{i}") for i in range(2)]
        scored, exp_done, pv_done, spread, o_copied, o_logged, o_rinv, attn_done = (sem(n) for n in (
            "scored", "exp_done", "pv_done", "spread", "o_copied", "o_logged", "o_rinv", "attn_done"))
        fw_pool, b_built = sem("fw_pool"), sem("b_built")
        up_mm, gelu_done = sem("up_mm"), sem("gelu_done")
        comb_done, combT_done = sem("comb_done"), sem("combT_done")
        gate_mm, silu_done, prod_done, hid_done = sem("gate_mm"), sem("silu_done"), sem("prod_done"), sem("hid_done")
        hid_used, moe_added = sem("hid_used"), sem("moe_added")
        dve_self, pool_self = sem("dve_self"), sem("pool_self")
        stored = sem("stored")

        UP_BANKS = (SB[:, 0, 0, :], SB[:, 0, 1, :], OB[:, :], GB[:, :])

        def chunk(c):
            return slice(c * CH, (c + 1) * CH)

        PROJ = [(0, 1, 0), (0, 0, 0), (0, 1, 1), (0, 0, 1), (1, 1, 0), (1, 0, 0), (1, 1, 1), (1, 0, 1)]
        NORM = [(0, 0), (0, 1), (1, 0), (2, 0), (1, 1), (2, 1), (3, 0), (3, 1)]

        def unit(U):
            l, u = divmod(U, UPL)
            return l, u // 2, u % 2

        def queries(b):
            return slice(b * SEQ, (b + 1) * SEQ)

        UNITS = LAYERS * UPL
        def maxima(U, *which):
            return [("maximum", U, i) for i in which]

        EXTRA = {
            0: {(0, "first"): maxima(1, 4, 5, 6, 7), (0, "late"): [("stack", 3)]},
            1: {(3, "late"): [("fw", 0)]},
            2: {(1, "late"): [("fw", 1)], (3, "late"): [("fw", 2)]},
            3: {(3, "late"): [("fw", 3)]},
            4: {(3, "late"): [("out", 0, 0)]},
            5: {(0, "early"): [("centre", 2)], (1, "early"): [("average", 2)], (1, "late"): [("normed", 2)],
                (2, "late"): [("up", 0)], (3, "late"): [("down", 0)]},
            6: {(0, "early"): [("centre", 3)], (1, "early"): [("average", 3)],
                (1, "late"): [("normed", 3), ("project", 4)],
                (2, "late"): [("project", 5), ("stack", 4), ("stack", 5)], (3, "late"): [("values", 0)]},
            7: {(0, "late"): [("project", 6)]},
            8: {(0, "first"): maxima(9, 5, 6, 7), (0, "early"): [("centre", 4)], (1, "early"): [("average", 4)],
                (1, "late"): [("normed", 4)], (2, "late"): [("up", 1)], (3, "late"): [("down", 1)]},
            9: {(0, "early"): [("centre", 5)], (1, "early"): [("average", 5)], (1, "late"): [("normed", 5)],
                (2, "late"): [("project", 7)], (3, "late"): [("values", 1)]},
            10: {(0, "late"): [("stack", 7)]},
            11: {(0, "late"): maxima(12, 0, 1, 2, 3), (1, "early"): maxima(12, 4, 5, 6, 7), (1, "late"): [("turn", 12)],
                 (2, "late"): maxima(13, 0, 1, 2, 3), (3, "late"): maxima(13, 4, 5, 6, 7)},
            12: {(2, "late"): [("out", 1, 0)]},
            13: {(0, "early"): [("centre", 6)], (1, "early"): [("average", 6)], (1, "late"): [("normed", 6)],
                 (2, "late"): [("logits", 0)]},
            14: {(1, "late"): [("routing", 0)]},
            15: {(0, "late"): [("comb", 0)]},
        }
        LATE_TURN = (5, 8, 13)
        PLAN = {(U, k): [] for U in range(UNITS + 1) for k in range(-1, 4)}

        for U in range(UNITS):
            extra = EXTRA.get(U, {})
            later = U + 2 if U + 2 < UNITS and U + 2 not in (8, 9, 12, 13) else None
            for k in range(4):
                m = maxima(later, 2 * k, 2 * k + 1) if later else []
                steps = PLAN[U, k]
                steps += extra.get((k, "first"), []) + m[0:1] + extra.get((k, "early"), [])
                if k == 1 and U and U not in (8, 12):
                    steps += [("weighted", U - 1, 1)]
                if k == 3:
                    steps += [("weighted", U, 0)]
                if k == 1 and U in LATE_TURN:
                    steps += [("turn", U + 1)]
                steps += m[1:]
                if k == 0 and U not in LATE_TURN and U + 1 < UNITS and U + 1 not in (8, 12):
                    steps += [("turn", U + 1)]
                if k == 2 and U and U not in (8, 12):
                    steps += [("invert", U - 1)]
                steps += extra.get((k, "late"), [])
        ALL = range(8)
        PLAN[0, -1] = maxima(0, *ALL) + [("turn", 0), ("project", 3)] + maxima(1, 0, 1, 2, 3)
        PLAN[8, -1] = [("weighted", 7, 1), ("invert", 7)] + maxima(8, *ALL) + [("turn", 8)] + maxima(9, 0, 1) + \
            [("out", 0, 1, (0,))] + maxima(9, 2) + [("out", 0, 1, (1,))] + maxima(9, 3) + \
            [("out", 0, 1, (2,))] + maxima(9, 4) + [("out", 0, 1, (3,)), ("stack", 6)]
        PLAN[12, -1] = [("weighted", 11, 1), ("invert", 11)]
        PLAN[UNITS, -1] = [("weighted", UNITS - 1, 1), ("invert", UNITS - 1)]

        def up_at(c):
            return next(point[0] for point, steps in PLAN.items() if ("up", c) in steps)

        def do_plan(engine_steps, pair=None):
            for (U, k), steps in PLAN.items():
                if pair and U < UNITS and k >= 0:
                    pair(U, k)
                for step, *args in steps:
                    if step in engine_steps:
                        engine_steps[step](*args)

        gb_no = {}

        block = ctx.enter_context(nc.Block())

        @block.tensor
        def _(pe):
            CENTRE, MEAN, EYE = (cst[:, i, :] for i in range(3))

            def mm(out, lhsT, rhs, start=True, stop=True):
                return nc.tensor.matmul(out, lhsT, rhs, start=start, stop=stop)

            def take_gb(*step):
                if gb_no:
                    pe.wait_ge(gb_read, len(gb_no))
                gb_no[step] = len(gb_no) + 1

            def centre(n):
                s, c = NORM[n]
                take_gb("centre", n)
                if s == 0:
                    pe.wait_ge(x_in[c], 16)
                    pe.wait_ge(cst_in, 16)
                mm(GB[:, :], CENTRE, x[:, chunk(c)]).then_inc(gb_made, 1)

            def average(n):
                s, c = NORM[n]
                take_gb("average", n)
                pe.wait_ge(squared, n + 1)
                mm(GB[:, :], MEAN, sq[:, c, :]).then_inc(gb_made, 1)

            def project_first_keys(c):
                if c == 0:
                    pe.wait_ge(wqkv_in, 16)
                else:
                    pe.wait_ge(k_read, 1)
                pe.wait_ge(cx_in[c], 16)
                mm(OB[:, :], w_qkv[:, 0, 1, :], cx[:, chunk(c)]).then_inc(k_projected, 1)

            def project(m):
                l, is_k, c = PROJ[m]
                take_gb("project", m)
                if not is_k:
                    pe.wait_ge(xn_done, NORM.index((2 * l, c)) + 1)
                src = cx if is_k else xn
                mm(GB[:, :], w_qkv[:, l, is_k, :], src[:, chunk(c)]).then_inc(gb_made, 1)

            def value_products(bank, l, c):
                for t in range(4):
                    at = c * CH + t * D
                    last = mm(bank[:, D * t:D * t + D], cx[:, at:at + D], w_qkv[:, l, 2, :])
                return last

            def next_values(c):
                take_gb("values", c)
                value_products(GB, 1, c).then_inc(gb_made, 1)

            def maxima(U, i):
                l, b, g = unit(U)
                k, qt = divmod(i, 2)
                p = 4 * g + k
                if i == 0 and U % 4 == 0:
                    c = b // 2
                    pe.wait_ge(stacked[PROJ.index((l, 1, c))], 2 * 16)
                    pe.wait_ge(stacked[PROJ.index((l, 0, c))], (2 + 2 * l) * 16)
                    if U == 0:
                        pe.wait_ge(fixed_in, 4 * 16)
                        pe.wait_ge(k_zero0, 2)
                    if U == 4:
                        pe.wait_ge(k_zero1, 2)
                if 8 * U + i >= 2:
                    pe.wait_ge(max_red, 8 * U + i - 1)
                elif i == 0:
                    pe.wait_ge(v_done, 2)
                q0 = b * SEQ + qt * D
                mm(MB[:, i % 2, :].rearrange("p (h s) -> p h s", h=2), Q[:, p, q0:q0 + D],
                   K[:, :, p, queries(b)]).then_inc(max_mm, 1)

            def turn(U):
                take_gb("turn", U)
                pe.wait_ge(max_red, 8 * (U + 1))
                for qt in range(2):
                    last = mm(GB[0:8, D * qt:D * qt + D], nm[:, U % 2, qt, :], EYE)
                last.then_inc(gb_made, 1)

            ups = []

            def scores(U, k):
                l, b, g = unit(U)
                i = 4 * U + k
                if k == 0:
                    pe.wait_ge(shift_in[U % 2], 64 * (U // 2 + 1))
                if i >= 2:
                    pe.wait_ge(exp_done, i - 1)
                if ups and i % 2 == 0:
                    pe.wait_ge(gelu_done, 3 * len(ups))
                for kt in range(2):
                    s0 = b * SEQ + kt * D
                    for hh in range(2):
                        last = mm(SB[:, i % 2, kt, hh * SEQ:(hh + 1) * SEQ], K[:, hh, 4 * g + k, s0:s0 + D],
                                  Q[:, 4 * g + k, queries(b)])
                last.then_inc(scored, 1)

            def weighted(U, half):
                l, b, g = unit(U)
                pe.wait_ge(exp_done, 4 * U + 2 * half + 2)
                if half == 0 and U:
                    pe.wait_ge(o_copied, U)
                    if ups:
                        pe.wait_ge(gelu_done, 3 * len(ups))
                for kt in range(2):
                    for j in range(4):
                        k, hh = 2 * half + j // 2, j % 2
                        h = 2 * (4 * g + k) + hh
                        last = mm(OB[32 * j:32 * j + 32, half * SEQ:(half + 1) * SEQ], V[:, 2 * b + kt, h, :],
                                  P[:, (4 * U + k) % 4, kt, hh, :], start=kt == 0, stop=kt == 1)
                last.then_inc(pv_done, 1)

            def out_project(l, c, parts=range(4)):
                for i in parts:
                    if i == 0:
                        take_gb("out", l, c)
                        pe.wait_ge(attn_done, UPL * l + 4 * c + 4)
                        if l == 0 and c == 0:
                            pe.wait_ge(wo_in, 16)
                    last = mm(GB[:, :], w_o[:, l, i, :], attn[:, i, chunk(c)], start=i == 0, stop=i == 3)
                    if i == 3:
                        last.then_inc(gb_made, 1)

            def fw(step):
                take_gb("fw", step)
                if step == 0:
                    pe.wait_ge(fw_pool, 1)
                    for b in range(BLK):
                        last = mm(GB[:, D * b:D * b + D], e_up[:, b, EDGE - D:EDGE], w_exp[:, b, 0:D])
                elif step == 1:
                    for b in range(BLK):
                        last = mm(GB[:, b:b + 1], e_up[:, b, EDGE - D:EDGE], w_exp[:, b, D:D + 1])
                elif step == 2:
                    pe.wait_ge(fw_pool, 2)
                    for b in range(BLK):
                        last = mm(GB[:, D * b:D * b + D], e_dn[:, b, EDGE - D:EDGE], w_con[:, b, :])
                else:
                    pe.wait_ge(fw_pool, 3)
                    for b in range(BLK):
                        last = mm(GB[:, D * b:D * b + D], g_up[:, b, 0:D], EYE)
                last.then_inc(gb_made, 1)

            def up(c):
                take_gb("up", c)
                pe.wait_ge(xn_done, NORM.index((1, c)) + 1)
                pe.wait_ge(exp_done, 4 * up_at(c) + 3)
                for k in range(BLK):
                    if k == 2:
                        pe.wait_ge(o_copied, up_at(c))
                    mm(UP_BANKS[k], w_up[:, k, :], xn[:, chunk(c)])\
                        .then_inc(up_mm if k < BLK - 1 else gb_made, 1)
                ups.append(c)

            def down(c):
                take_gb("down", c)
                pe.wait_ge(gelu_done, 3 * c + 3)
                for k in range(BLK):
                    last = mm(GB[:, :], w_dn[:, k, :], attn[:, k, chunk(c)], start=k == 0, stop=k == BLK - 1)
                last.then_inc(gb_made, 1)

            def router_logits(c):
                take_gb("logits", c)
                pe.wait_ge(moe_in, 7 * 16)
                pe.wait_ge(xn_done, NORM.index((3, c)) + 1)
                for t in range(4):
                    at = c * CH + t * D
                    last = mm(GB[:, 16 * t:16 * t + 16], xn[:, at:at + D], w_g[:, :])
                last.then_inc(gb_made, 1)

            def turn_weights(c):
                take_gb("comb", c)
                pe.wait_ge(comb_done, c + 1)
                for t in range(4):
                    last = mm(GB[0:16, D * t:D * t + D], route[:, 6 + c, t, :], EYE)
                last.then_inc(gb_made, 1)

            steps = {"centre": centre, "average": average, "project": project, "values": next_values,
                     "out": out_project, "fw": fw, "up": up, "down": down, "logits": router_logits,
                     "comb": turn_weights, "maximum": maxima, "turn": turn, "weighted": weighted}

            centre(0)
            project_first_keys(0)
            average(0)
            project(1)
            project_first_keys(1)
            centre(1)
            for c in range(NCH):
                value_products(MB[:, c, :], 0, c).then_inc(v_mm, 1)
            average(1)
            pe.wait_ge(k_read, 2)
            do_plan(steps, scores)

            beside = {0: (out_project, 1, 1), 1: (centre, 7), 2: (average, 7), 3: (router_logits, 1), 6: (turn_weights, 1)}
            pe.wait_ge(exp_done, 4 * UPL * LAYERS)
            pe.wait_ge(max_red, 8 * UPL * LAYERS)

            for c in range(NCH):
                pe.wait_ge(combT_done, 2 * (c + 1))

                def down_product(e):
                    i = (EPAIRS + 1) * c + e
                    rows = D if e < EPAIRS else INTER
                    if i == 0:
                        pe.wait_ge(o_copied, UPL * LAYERS)
                    if e == 0 and c:
                        pe.wait_ge(moe_added, c)
                    if e < EPAIRS:
                        pe.wait_ge(hid_done, EPAIRS * c + e + 1)
                    else:
                        pe.wait_ge(prod_done, i + 1)
                    w = w_2[:, e, :] if e < EPAIRS else w_2s[INTER:D, :]
                    mm(OB[:, :], w, hid_t[D - rows:D, i % 2, :], start=e == 0, stop=e == EPAIRS).then_inc(hid_used, 1)

                for e in range(EPAIRS + 1):
                    i = (EPAIRS + 1) * c + e
                    if i >= 2:
                        pe.wait_ge(prod_done, i - 1)
                        pe.wait_ge(hid_done, EPAIRS * c + e - 1 if e else EPAIRS * c)
                    for j in range(2 if e < EPAIRS else 1):
                        w = w_gu[:, e, j, :] if e < EPAIRS else w_gus[:, :]
                        last = mm(SB[:, i % 2, j, :], w, xn[:, chunk(c)])
                    if e < EPAIRS:
                        last = mm(MB[:, i % 2, :], selt[:, e, :], combT[:, c, :])
                    last.then_inc(gate_mm, 1)
                    if c == 0 and e in beside:
                        step, *args = beside[e]
                        step(*args)
                    if e:
                        down_product(e - 1)
                down_product(EPAIRS)

        @block.sync
        def _(sp):
            def send_terms(m):
                is_k = PROJ[m][1]
                sp.wait_ge(split_done, m + 1)
                t = terms[:, m % 2, :, :]
                if is_k:
                    parts = ((0, 3, t), (3, 5, t[:, 0:2, :]), (5, 6, t[:, 0:1, :]))
                else:
                    parts = ((0, 3, t[:, 0:1, :].broadcast_to([D, 3, CH])),
                             (3, 5, t[:, 1:2, :].broadcast_to([D, 2, CH])), (5, 6, t[:, 2:3, :]))
                for t0, t1, src in parts:
                    sp.dma_start(bounce[m, t0:t1, :, :].rearrange("t r n -> r t n"), src).then_inc(bounced[m], 16)

            def stack(m):
                l, is_k, c = PROJ[m]
                sp.wait_ge(bounced[m], 48)
                if l:
                    sp.wait_ge(scored, 4 * 4 * (c + 1))
                for hh in range(2):
                    dst = K[64 * hh:64 * hh + SHIFT, hh, :, chunk(c)] if is_k \
                        else Q[64 * hh:64 * hh + SHIFT, :, chunk(c)]
                    src = bounce[m, :, 64 * hh:64 * hh + 64, :].rearrange("t (d p) n -> t d p n", d=DH)
                    sp.dma_start(dst, src).then_inc(stacked[m], 16)
                if l and not is_k:
                    for hh in range(2):
                        sp.dma_start(Q[64 * hh + SHIFT:64 * hh + SHIFT + 2, :, chunk(c)].bitcast(u16),
                                     fixed[1, 0:PAIRS * CH].rearrange("(p n) -> p n", p=PAIRS)
                                     .partition_broadcast(2)).then_inc(stacked[m], 16)

            def shift_rows(U):
                l, b, g = unit(U)
                sp.wait_ge(gb_read, gb_no["turn", U])
                for hh in range(2):
                    for t in range(2):
                        row = 64 * hh + SHIFT + t
                        sp.dma_start(Q[row:row + 1, 4 * g:4 * g + 4, queries(b)], nmT[4 * hh:4 * hh + 4, U % 2, t, :])\
                            .then_inc(shift_in[U % 2], 16)

            sp.dma_start(x[:, chunk(0)], xT[:, chunk(0)]).then_inc(x_in[0], 16)
            sp.dma_start(cx[:, chunk(0)], ctxT[:, chunk(0)]).then_inc(cx_in[0], 16)
            sp.dma_start(x[:, chunk(1)], xT[:, chunk(1)]).then_inc(x_in[1], 16)
            sp.dma_start(cx[:, chunk(1)], ctxT[:, chunk(1)]).then_inc(cx_in[1], 16)
            for hh in range(2):
                sp.dma_start(K[64 * hh + SHIFT:64 * hh + 64, hh, :, :].bitcast(u16),
                             fixed[0].rearrange("(p n) -> p n", p=PAIRS).partition_broadcast(64 - SHIFT))\
                    .then_inc(fixed_in, 16)
                sp.dma_start(Q[64 * hh + SHIFT:64 * hh + 64, :, :].bitcast(u16),
                             fixed[1].rearrange("(p n) -> p n", p=PAIRS).partition_broadcast(64 - SHIFT))\
                    .then_inc(fixed_in, 16)
            sp.dma_start(bvb[:, :, :], bv.rearrange("l d -> (l d)").partition_broadcast(D)).then_inc(bv_in, 16)
            send_terms(0)
            send_terms(1)
            stack(0)
            stack(1)
            send_terms(2)
            stack(2)
            do_plan({"project": send_terms, "stack": stack, "turn": shift_rows})
            for c in range(NCH):
                sp.wait_ge(moe_added, c + 1)
                sp.dma_start(outT[:, chunk(c)], x[:, chunk(c)]).then_inc(stored, 16)
            sp.wait_ge(stored, 16 * NCH)

        @block.gpsimd
        def _(pool):
            steps = [0]

            def link(ins):
                steps[0] += 1
                ins.then_inc(pool_self, 1)
                pool.wait_ge(pool_self, steps[0])

            for hh in range(2):
                nc.gpsimd.memset(K[64 - 64 * hh:128 - 64 * hh, hh, :, chunk(1)].bitcast(u32), 0).then_inc(k_zero1, 1)
                pool.wait_ge(k_zero1, hh + 1)
            nc.gpsimd.memset(V[:, :, :, DH:32], 1.0).then_inc(v_ones, 1)
            pool.wait_ge(v_ones, 1)
            nc.gpsimd.memset(combT[:, :, :].bitcast(u32), 0).then_inc(comb_zero, 1)
            pool.wait_ge(comb_zero, 1)
            pool.wait_ge(stacked[1], 2 * 16)
            for dst, src in ((e_up[:, :, :], eup), (e_dn[:, :, :], edn), (mixc[:, :, :, :, :], mix),
                             (w_exp[:, :, :], wexp), (w_con[:, :, :], wcon)):
                pool.dma_start(dst, src).then_inc(ffn_in, 16)
            pool.dma_start(w_o[:, :, :, :], woq).then_inc(wo_in, 16)

            pool.wait_ge(ffn_in, 5 * 16)
            for s in range(1, 7):
                w = 2 ** s
                at = 2 * w - 2
                old = e_up[:, :, at - w:at].unsqueeze(2).broadcast_to([D, BLK, 2, w])
                new = e_up[:, :, at:at + 2 * w].rearrange("p b (o i) -> p b o i", o=2)
                link(nc.gpsimd.tensor_tensor(new, new, old, ALU.mult))
            for s in range(1, 7):
                w = 2 ** s
                at = 2 * w - 2
                old = e_dn[:, :, at - w:at].unsqueeze(3).broadcast_to([D, BLK, w, 2])
                new = e_dn[:, :, at:at + 2 * w].rearrange("p b (i o) -> p b i o", o=2)
                ins = nc.gpsimd.tensor_tensor(new, new, old, ALU.mult)
                if s < 6:
                    link(ins)
            ins.then_inc(fw_pool, 1)

            def mix_blocks(k, low, dst, src, n):
                s4 = src.rearrange("p (h l) n -> p h l n", h=2)
                d4 = dst.rearrange("p (h l) n -> p h l n", h=2)
                for i, t in ((0, mix_a), (1, mix_b)):
                    s = s4[:, :, i:i + 1, :] if low else s4[:, i:i + 1, :, :]
                    t4 = t[:, :, 0:n].rearrange("p (h l) n -> p h l n", h=2)
                    cc = mixc[:, k, :, :, i:i + 1].broadcast_to([D, 2, 2, n])
                    ins = nc.gpsimd.tensor_tensor(t4, s.broadcast_to([D, 2, 2, n]), cc, ALU.mult)
                    link(ins)
                return nc.gpsimd.tensor_tensor(d4, mix_a[:, :, 0:n].rearrange("p (h l) n -> p h l n", h=2),
                                               mix_b[:, :, 0:n].rearrange("p (h l) n -> p h l n", h=2), ALU.add)

            link(mix_blocks(2, False, w_con[:, :, :], w_con[:, :, :], D))
            mix_blocks(3, True, w_con[:, :, :], w_con[:, :, :], D).then_inc(fw_pool, 1)

            def normalise(U):
                l, b, g = unit(U)
                pool.wait_ge(o_rinv, U + 1)
                if l and U % 4 == 0:
                    pool.wait_ge(gb_read, gb_no["down", b // 2])
                nc.gpsimd.tensor_tensor(attn[:, 2 * g:2 * g + 2, queries(b)],
                                        o_raw[:, U % 2, :].rearrange("p (h q) -> p h q", h=2),
                                        rinv[:, U % 2, :].rearrange("p (h q) -> p h q", h=2),
                                        ALU.mult).then_inc(attn_done, 1)

            def load_experts():
                for dst, src in ((w_gu[:, :, :, :], gu), (w_2[:, :, :], w2p), (w_gus[:, :], gus), (w_2s[INTER:D, :], w2s),
                                 (w_g[:, :], gwT), (selt[:, :, :].bitcast(u16), sel),
                                 (gbb[:, :], gate_b.partition_broadcast(D))):
                    pool.dma_start(dst, src).then_inc(moe_in, 16)

            def mix_up():
                pool.wait_ge(gb_read, gb_no["fw", 1])
                pool.wait_ge(fw_pool, 2)
                link(mix_blocks(0, True, g_up[:, :, :], g_up[:, :, :], D + 1))
                mix_blocks(1, False, g_up[:, :, :], g_up[:, :, :], D + 1).then_inc(fw_pool, 1)

            def after_weighted(U, half):
                if half:
                    normalise(U)
                    if U == 1:
                        mix_up()
                        load_experts()

            do_plan({"weighted": after_weighted})

        @block.scalar
        def _(act):
            act.dma_start(cst[:, :, :], consts).then_inc(cst_in, 16)
            act.dma_start(w_qkv[:, :, :, :], wqkv).then_inc(wqkv_in, 16)
            act.dma_start(col[:, :], cols).then_inc(col_in, 16)

            def square(n):
                c = NORM[n][1]
                act.wait_ge(gb_made, gb_no["centre", n])
                nc.scalar.activation(sq[:, c, :], GB[:, :], ACT.Square).then_inc(squared, 1)
                nc.scalar.activation(xn[:, chunk(c)], GB[:, :], ACT.Copy).then_inc(gb_read, 1)

            def rstd_of(n):
                c = NORM[n][1]
                act.wait_ge(gb_made, gb_no["average", n])
                nc.scalar.activation(rstd[:, c, :], GB[:, :], ACT.Ln, bias=eps[:, 0:1]).then_inc(gb_read, 1)
                act.wait_ge(gb_read, gb_no["average", n])
                nc.scalar.activation(rstd[:, c, :], rstd[:, c, :], ACT.Exp, scale=-0.5).then_inc(rstd_done, 1)

            def exps(U, k):
                i = 4 * U + k
                act.wait_ge(scored, i + 1)
                if i >= 4:
                    act.wait_ge(pv_done, (i - 4) // 2 + 1)
                nc.scalar.activation(P[:, i % 4, :, :, :].rearrange("p k h q -> p (k h q)"),
                                     SB[:, i % 2, :, :].rearrange("p k n -> p (k n)"),
                                     ACT.Exp, scale=SCALE).then_inc(exp_done, 1)

            def invert(U):
                act.wait_ge(spread, U + 1)
                if U >= 2:
                    act.wait_ge(attn_done, U - 1)
                nc.scalar.activation(o_raw[:, U % 2, :], OB[:, :], ACT.Copy).then_inc(o_copied, 1)
                nc.scalar.activation(rinv[:, U % 2, :], sums[:, U % 2, :], ACT.Ln).then_inc(o_logged, 1)
                act.wait_ge(o_logged, U + 1)
                nc.scalar.activation(rinv[:, U % 2, :], rinv[:, U % 2, :], ACT.Exp, scale=-1.0).then_inc(o_rinv, 1)

            def gelu(c):
                act.preload_act_table_set(GELU)
                for k in range(BLK):
                    if k < BLK - 1:
                        act.wait_ge(up_mm, 3 * c + k + 1)
                    else:
                        act.wait_ge(gb_made, gb_no["up", c])
                    nc.scalar.activation(attn[:, k, chunk(c)], UP_BANKS[k], ACT.Gelu,
                                         bias=b_up[:, k:k + 1]).then_inc(gelu_done if k < BLK - 1 else gb_read, 1)
                act.preload_act_table_set(EXP_LN)

            def router_exp(c):
                act.wait_ge(gb_made, gb_no["logits", c])
                nc.scalar.activation(route[:, c, :, :], GB[:, 0:64].rearrange("p (t e) -> p t e", e=EXPERTS),
                                     ACT.Exp, scale=-1.0).then_inc(gb_read, 1)

            steps = {"centre": square, "average": rstd_of, "up": gelu, "logits": router_exp,
                     "invert": invert}

            act.preload_act_table_set(EXP_LN)
            act.wait_ge(eps_set, 1)
            square(0)
            rstd_of(0)
            square(1)
            rstd_of(1)
            do_plan(steps, exps)
            beside = {1: (square, 7), 2: (rstd_of, 7), 3: (router_exp, 1)}
            for c in range(NCH):
                for e in range(EPAIRS + 1):
                    i = (EPAIRS + 1) * c + e
                    rows = D if e < EPAIRS else INTER
                    if i == 0:
                        act.preload_act_table_set(SILU)
                    act.wait_ge(gate_mm, i + 1)
                    if i >= 2:
                        act.wait_ge(prod_done, i - 1)
                    nc.scalar.activation(gate_t[D - rows:D, i % 2, :], SB[0:rows, i % 2, 0, :], ACT.Silu).then_inc(silu_done, 1)
                    if c == 0 and e in beside:
                        step, *args = beside[e]
                        if step == rstd_of:
                            act.preload_act_table_set(EXP_LN)
                        step(*args)
                        if step == router_exp:
                            act.preload_act_table_set(SILU)

        @block.vector
        def _(dve):
            links = [0]

            def link(ins):
                links[0] += 1
                ins.then_inc(dve_self, 1)
                dve.wait_ge(dve_self, links[0])

            def split(m):
                l, is_k, c = PROJ[m]
                bank = OB if (l, is_k) == (0, 1) else GB
                bias = col[:, (BK if is_k else BQ) + l:(BK if is_k else BQ) + l + 1]
                t = terms[:, m % 2, :, :]
                r = rest[:, m % 2, :]
                if bank is OB:
                    dve.wait_ge(k_projected, c + 1)
                else:
                    dve.wait_ge(gb_made, gb_no["project", m])
                if m == 0:
                    dve.wait_ge(col_in, 16)
                if m >= 2:
                    dve.wait_ge(bounced[m - 2], 48)
                link(nc.vector.tensor_scalar(t[:, 0, :], bank[:, :], bias, None, ALU.add))
                read = nc.vector.scalar_tensor_tensor(r, bank[:, :], bias, t[:, 0, :], ALU.add, ALU.subtract)
                if bank is OB:
                    read.then_inc(k_read, 1)
                    dve.wait_ge(k_read, c + 1)
                else:
                    read.then_inc(gb_read, 1)
                    dve.wait_ge(gb_read, gb_no["project", m])
                link(nc.vector.tensor_copy(t[:, 1, :], r))
                nc.vector.tensor_tensor(t[:, 2, :], r, t[:, 1, :], ALU.subtract).then_inc(split_done, 1)

            def normed(n):
                c = NORM[n][1]
                dve.wait_ge(rstd_done, n + 1)
                nc.vector.tensor_tensor(xn[:, chunk(c)], xn[:, chunk(c)], rstd[:, c, :], ALU.mult).then_inc(xn_done, 1)

            def add_value_bias(l, c, bank):
                bias = bvb[:, l, :].rearrange("p (h d) -> p h d", d=DH)
                for t in range(4):
                    last = nc.vector.tensor_tensor(V[:, 4 * c + t, :, 0:DH],
                                                   bank[:, D * t:D * t + D].rearrange("p (h d) -> p h d", d=DH),
                                                   bias, ALU.add)
                return last

            def first_values(c):
                dve.wait_ge(v_mm, c + 1)
                if c == 0:
                    dve.wait_ge(bv_in, 16)
                    dve.wait_ge(v_ones, 1)
                add_value_bias(0, c, MB[:, c, :]).then_inc(v_done, 1)

            def next_values(c):
                dve.wait_ge(gb_made, gb_no["values", c])
                dve.wait_ge(pv_done, 2 * 4 * (c + 1))
                add_value_bias(1, c, GB).then_inc(gb_read, 1)

            def reduce(U, i):
                k, qt = divmod(i, 2)
                dve.wait_ge(max_mm, 8 * U + i + 1)
                nc.vector.tensor_reduce(nm[:, U % 2, qt, k:8:4], MB[:, i % 2, :].rearrange("p (h s) -> p h s", h=2),
                                        AX.X, ALU.max, negate=True).then_inc(max_red, 1)

            def split_max(U):
                dve.wait_ge(gb_made, gb_no["turn", U])
                if U >= 2:
                    dve.wait_ge(shift_in[U % 2], 64 * (U // 2))
                link(nc.vector.tensor_copy(nmT[:, U % 2, 0, :], GB[0:8, 0:SEQ]))
                nc.vector.tensor_tensor(nmT[:, U % 2, 1, :], GB[0:8, 0:SEQ], nmT[:, U % 2, 0, :],
                                        ALU.subtract).then_inc(gb_read, 1)

            def spread_sums(U):
                dve.wait_ge(pv_done, 2 * (U + 1))
                if U >= 2:
                    dve.wait_ge(attn_done, U - 1)
                nc.vector.stream_shuffle(sums[:, U % 2, :], OB[:, :], [DH] * 32).then_inc(spread, 1)

            def residual(c, bias, *step):
                dve.wait_ge(gb_made, gb_no[step])
                nc.vector.scalar_tensor_tensor(x[:, chunk(c)], GB[:, :], bias, x[:, chunk(c)],
                                               ALU.add, ALU.add).then_inc(gb_read, 1)

            def add_attention(l, c, parts=(3,)):
                if 3 in parts:
                    residual(c, col[:, BO + l:BO + l + 1], "out", l, c)

            def add_ffn(c):
                dve.wait_ge(b_built, 1)
                residual(c, b_dn[:, 0:1], "down", c)

            def fw_read(step):
                dve.wait_ge(gb_made, gb_no["fw", step])
                if step == 1:
                    dst, src = g_up[:, :, D:D + 1], GB[:, 0:BLK].unsqueeze(2)
                else:
                    dst = (g_up[:, :, 0:D], None, w_dn[:, :, :], w_up[:, :, :])[step]
                    src = GB[:, :].rearrange("p (b n) -> p b n", b=BLK)
                if step == 3:
                    nc.vector.tensor_tensor(b_dn[:, :], col[:, BCON:BCON + 1], col[:, BDOWN:BDOWN + 1], ALU.add)\
                        .then_inc(b_built, 1)
                    link(nc.vector.tensor_tensor(b_up[:, :], g_up[:, :, D:D + 1].rearrange("p b o -> p (b o)"),
                                                 col[:, BUP:BUP + BLK], ALU.add))
                nc.vector.tensor_copy(dst, src).then_inc(gb_read, 1)

            def routing(c):
                ex, sc, bi, le, ws = (route[:, i, :, :] for i in (c, 2, 3, 4, 5))
                dve.wait_ge(gb_read, gb_no["logits", c])
                link(nc.vector.tensor_scalar(ex, ex, 1.0, None, ALU.add))
                link(nc.vector.reciprocal(sc, ex))
                link(nc.vector.tensor_tensor(bi, sc, gbb[:, :].unsqueeze(1).broadcast_to([D, 4, EXPERTS]), ALU.add))
                for t in range(4):
                    ins = nc.vector.max(top[:, t, :], bi[:, t, :])
                link(ins)
                link(nc.vector.memset(top[:, :, TOPK:8], -3.0e38))
                for t in range(4):
                    ins = nc.vector.match_replace(out=le[:, t, :], in_to_replace=top[:, t, :], in_values=bi[:, t, :],
                                                  imm_value=-1.0e38)
                link(ins)
                link(nc.vector.tensor_tensor(le, le, bi, ALU.not_equal))
                link(nc.vector.tensor_tensor(ws, sc, le, ALU.mult))
                link(nc.vector.reduce_sum(rsum[:, 0, :], ws, AX.X))
                link(nc.vector.reciprocal(rsum[:, 1, :], rsum[:, 0, :]))
                nc.vector.scalar_tensor_tensor(route[:, 6 + c, :, :], ws, ROUTE_SCALE,
                                               rsum[:, 1, :].unsqueeze(2).broadcast_to([D, 4, EXPERTS]),
                                               ALU.mult, ALU.mult).then_inc(comb_done, 1)

            def weight_terms(c):
                dve.wait_ge(gb_made, gb_no["comb", c])
                dve.wait_ge(comb_zero, 1)
                link(nc.vector.tensor_copy(combT[0:16, c, :], GB[0:16, :]))
                if c:
                    dve.wait_ge(combT_done, 2 * c)
                nc.vector.tensor_tensor(crest[:, :], GB[0:16, :], combT[0:16, c, :], ALU.subtract).then_inc(gb_read, 1)
                dve.wait_ge(gb_read, gb_no["comb", c])
                link(nc.vector.tensor_copy(cterm[:, 0, :], crest[:, :]))
                link(nc.vector.tensor_tensor(cterm[:, 1, :], crest[:, :], cterm[:, 0, :], ALU.subtract))
                nc.vector.tensor_copy(combT[32:48, c, :], cterm[:, 0, :]).then_inc(combT_done, 1)
                nc.vector.tensor_copy(combT[64:80, c, :], cterm[:, 1, :]).then_inc(combT_done, 1)

            def after_weighted(U, half):
                if half:
                    spread_sums(U)

            def first_routing(c):
                dve.wait_ge(moe_in, 7 * 16)
                routing(c)

            steps = {"normed": normed, "project": split, "values": next_values,
                     "out": add_attention, "fw": fw_read, "down": add_ffn, "routing": first_routing,
                     "comb": weight_terms, "maximum": reduce, "turn": split_max, "weighted": after_weighted}

            nc.vector.memset(eps[:, :], EPS).then_inc(eps_set, 1)
            for hh in range(2):
                nc.vector.memset(K[64 - 64 * hh:128 - 64 * hh, hh, :, chunk(0)].bitcast(u32), 0).then_inc(k_zero0, 1)
            split(0)
            normed(0)
            split(1)
            split(2)
            for c in range(NCH):
                first_values(c)
            normed(1)
            do_plan(steps)
            beside = {0: (add_attention, 1, 1), 2: (normed, 7), 3: (routing, 1), 6: (weight_terms, 1)}
            for c in range(NCH):
                for e in range(EPAIRS + 1):
                    i = (EPAIRS + 1) * c + e
                    dve.wait_ge(silu_done, i + 1)
                    if i >= 2:
                        dve.wait_ge(hid_used, i - 1)
                    rows = slice(0 if e < EPAIRS else INTER, D)
                    dst, j = (prod_t, 1) if e < EPAIRS else (hid_t, 0)
                    nc.vector.tensor_tensor(dst[rows, i % 2, :], SB[rows, i % 2, j, :], gate_t[rows, i % 2, :],
                                            ALU.mult).then_inc(prod_done, 1)
                    if e < EPAIRS:
                        dve.wait_ge(prod_done, i + 1)
                        nc.vector.tensor_tensor(hid_t[:, i % 2, :], MB[:, i % 2, :], prod_t[:, i % 2, :],
                                                ALU.mult).then_inc(hid_done, 1)
                    if c == 0 and e in beside:
                        step, *args = beside[e]
                        step(*args)
                dve.wait_ge(hid_used, (EPAIRS + 1) * (c + 1))
                nc.vector.tensor_tensor(x[:, chunk(c)], OB[:, :], x[:, chunk(c)], ALU.add).then_inc(moe_added, 1)


_ORDER = ["xT", "ctxT", "wqkv", "woq", "cols", "mix", "bv", "gate_b", "wexp", "wcon", "eup", "edn", "gu", "gus",
          "w2p", "w2s", "gwT", "consts", "sel", "fixed"]


def _layout(inp):
    import numpy as np
    f = {k: np.asarray(v) for k, v in inp.items()}
    out = {}
    out["xT"] = f["x"].reshape(TOK, D).T
    out["ctxT"] = f["ctx_1024"].reshape(TOK, D).T
    perm = np.arange(D).reshape(PAIRS, 2, DH).transpose(1, 2, 0).reshape(-1)
    ws = []
    for l in range(LAYERS):
        q, k, v = (f[f"L{l}_xattn_W{n}"] for n in "qkv")
        if l == 0:
            q, k, v = q.T, k.T, v.T
        ws.append(np.stack([q[:, perm], k[:, perm], v], 1))
    out["wqkv"] = np.stack(ws, 1)
    wo = np.zeros((4, 32, LAYERS, 4, D), np.float32)
    for l in range(LAYERS):
        o = f[f"L{l}_xattn_Wo"]
        o = o.T if l == 0 else o
        wo[:, :DH, l] = o.reshape(4, 4, DH, D).transpose(1, 2, 0, 3)
    out["woq"] = wo.reshape(D, LAYERS, 4, D)
    vec = [f["L0_xattn_bq"][perm], f["L1_xattn_bq"][perm], f["L0_xattn_bk"][perm], f["L1_xattn_bk"][perm],
           f["L0_xattn_bo"], f["L1_xattn_bo"], f["L0_ffn_b_con"], f["L0_ffn_down_bias"]]
    vec += list(f["L0_ffn_up_bias"].reshape(BLK, D))
    out["cols"] = np.stack(vec, 1)
    up, dn = f["L0_ffn_up_weights"], f["L0_ffn_down_weights"]
    up7, dn7 = (w[7].reshape(2, D, 2, 2) for w in (up, dn))
    up8, dn8 = (w[8].reshape(2, D, 2, 2) for w in (up, dn))
    out["mix"] = np.stack([up7.transpose(1, 0, 2, 3), up8.transpose(1, 2, 0, 3),
                           dn8.transpose(1, 3, 0, 2), dn7.transpose(1, 0, 3, 2)], 1)
    out["bv"] = np.stack([f["L0_xattn_bv"], f["L1_xattn_bv"]])
    out["gate_b"] = f["L1_ffn_gate_b"]
    out["wexp"] = np.concatenate([f["L0_ffn_W_exp"].T, f["L0_ffn_b_exp"][:, None]], 1)\
        .reshape(BLK, D, D + 1).transpose(1, 0, 2)
    out["wcon"] = f["L0_ffn_W_con"].reshape(BLK, D, D).transpose(1, 0, 2)
    eu, ed = [], []
    for s in range(7):
        w = up[s].reshape(HID >> (s + 1), 2 ** s, 2, 2)
        w = w.transpose(0, 3, 2, 1).reshape(HID >> (s + 1), 2, 1, 2 ** (s + 1))
        eu.append(np.broadcast_to(w, (HID >> (s + 1), 2, 2 ** s, 2 ** (s + 1))).reshape(BLK, D, -1))
    for s in range(6, -1, -1):
        w = dn[s].reshape(BLK, 2 ** (6 - s), 2 ** s, 2, 2)
        w = w.transpose(3, 2, 0, 1, 4).reshape(1, 2 ** (s + 1), BLK, 2 ** (7 - s))
        ed.append(np.broadcast_to(w, (2 ** (6 - s), 2 ** (s + 1), BLK, 2 ** (7 - s))).reshape(D, BLK, -1))
    out["eup"] = np.concatenate(eu, 2).transpose(1, 0, 2)
    out["edn"] = np.concatenate(ed, 2)
    w13 = f["L1_ffn_w13"].reshape(EPAIRS, 2, 2, INTER, D)
    out["gu"] = w13.transpose(4, 0, 2, 1, 3).reshape(D, EPAIRS, 2, D)
    out["gus"] = f["L1_ffn_w13_s"].T
    out["w2p"] = f["L1_ffn_w2"].reshape(EPAIRS, 2, D, INTER).transpose(1, 3, 0, 2).reshape(D, EPAIRS, D)
    out["w2s"] = f["L1_ffn_w2_s"].T
    out["gwT"] = f["L1_ffn_gate_w"].T
    eye = np.eye(D, dtype=np.float32)
    mean = np.full((D, D), 1.0 / D, np.float32)
    out["consts"] = np.stack([eye - mean, mean, eye], 1)
    sel = np.zeros((3, 32, EPAIRS, 2, INTER), np.uint16)
    for e in range(EXPERTS):
        sel[:, e, e // 2, e % 2] = 0x3F80
    out["sel"] = sel.reshape(96, EPAIRS, D)[:80]
    out["fixed"] = np.repeat(np.array([0x3F80, 0], np.uint16), PAIRS * TOK).reshape(2, PAIRS * TOK)
    return {k: np.ascontiguousarray(v) for k, v in out.items()}


def kernel(**inputs):
    import numpy as np
    import concourse.bacc as bacc
    from concourse.bass_utils import run_bass_kernel_spmd

    nc = bacc.Bacc("TRN2", target_bir_lowering=False, num_devices=1)
    arrays = _layout(inputs)
    args = [nc.dram_tensor(n, arrays[n].shape, mybir.dt.from_np(arrays[n].dtype), kind="ExternalInput").ap()
            for n in _ORDER]
    args.append(nc.dram_tensor("outT", (D, TOK), mybir.dt.float32, kind="ExternalOutput").ap())
    build_program(nc, *args)
    r = run_bass_kernel_spmd(nc, [arrays], core_ids=[0])
    return np.ascontiguousarray(np.asarray(r.results[0]["outT"]).T).reshape(BATCH, SEQ, D)
```

```python
import concourse.bass as bass
from concourse import mybir
from contextlib import ExitStack

BATCH, SEQ, D = 4, 256, 128
TOK = BATCH * SEQ
HEADS, DH = 16, 8
PAIRS = HEADS // 2
CH = 512
NCH = TOK // CH
LAYERS = 2
UPL = 2 * BATCH
TERMS_Q = (0, 0, 0, 1, 1, 2)
TERMS_K = (0, 1, 2, 0, 1, 0)
SHIFT = DH * len(TERMS_Q)
HID = 512
BLK = HID // D
EDGE = 254
INTER = 64
EXPERTS = 16
EPAIRS = EXPERTS // 2
TOPK = 4
ROUTE_SCALE = 2.5
EPS = 1e-5
SCALE = DH ** -0.5
EXP_LN = "natural_log_exp_and_others"
GELU = "gelu_and_others"
SILU = "silu_and_others"
BQ, BK, BO, BCON, BDOWN, BUP, SECOND = 0, 2, 4, 6, 7, 8, 12
UNITS = LAYERS * UPL


def maxima(U, *which):
    return [("maximum", U, i) for i in which]


EXTRA = {
    (0, -1, "late"): maxima(0, 0, 1, 2, 3, 4, 5, 6, 7) + [("turn", 0)] + maxima(1, 0, 1, 2, 3, 4, 5, 6, 7),
    (0, 2, "late"): [("project", 3), ("split", 3)],
    (0, 3, "late"): [("stack", 3)],
    (1, 3, "late"): [("fw", 0)],
    (2, 1, "late"): [("fw", 1)],
    (2, 3, "late"): [("fw", 2)],
    (3, 3, "late"): [("fw", 3)],
    (4, 3, "late"): [("out", 0, 0)],
    (5, 0, "early"): [("centre", 2)],
    (5, 1, "early"): [("average", 2)],
    (5, 1, "late"): [("normed", 2)],
    (5, 2, "late"): [("up", 0)],
    (5, 3, "late"): [("down", 0), ("centre", 3)],
    (6, 0, "late"): [("project", 4), ("split", 4)],
    (6, 1, "early"): [("average", 3)],
    (6, 1, "late"): [("normed", 3)],
    (6, 2, "first"): [("project", 5), ("split", 5)],
    (6, 3, "first"): [("stack", 4)],
    (6, 3, "early"): [("values", 0)],
    (6, 3, "late"): [("stack", 5)],
    (7, 0, "late"): [("project", 6), ("split", 6)],
    (7, 3, "late"): maxima(8, 0),
    (8, -1, "late"): maxima(8, 1, 2, 3, 4, 5, 6, 7) + [("turn", 8)] + maxima(9, 0, 1, 2, 3)
    + [("out", 0, 1, (0,)), ("out", 0, 1, (1,))] + maxima(9, 4),
    (8, 0, "first"): maxima(9, 5) + [("out", 0, 1, (2,))] + maxima(9, 6) + [("out", 0, 1, (3,))] + maxima(9, 7),
    (8, 0, "early"): [("centre", 4)],
    (8, 1, "early"): [("average", 4)],
    (8, 2, "first"): [("normed", 4), ("stack", 6)],
    (8, 2, "late"): [("up", 1)],
    (8, 3, "first"): [("down", 1)],
    (8, 3, "late"): [("centre", 5)],
    (9, 1, "early"): [("average", 5)],
    (9, 1, "late"): [("normed", 5)],
    (9, 2, "late"): [("project", 7), ("split", 7)],
    (10, 1, "first"): [("stack", 7)],
    (10, 1, "late"): [("values", 1)],
    (11, 0, "late"): maxima(12, 0, 1, 2, 3, 4, 5),
    (11, 1, "early"): maxima(12, 6, 7),
    (11, 2, "early"): [("turn", 12)],
    (11, 2, "late"): maxima(13, 0, 1, 2),
    (11, 3, "early"): maxima(13, 3, 4),
    (11, 3, "late"): maxima(13, 5, 6),
    (12, -1, "late"): maxima(13, 7),
    (12, 2, "late"): [("out", 1, 0)],
    (12, 3, "late"): [("centre", 6)],
    (13, 0, "late"): [("average", 6)],
    (13, 1, "early"): [("normed", 6)],
    (13, 2, "early"): [("logits", 0)],
    (14, 2, "late"): [("routing", 0)],
    (15, 2, "first"): [("comb", 0)],
}
PLACED = (0, 1, 8, 9, 12, 13)
FLUSHED = (8, 12)
LATE_TURN = (1, 3, 5, 6, 8, 9, 10, 13, 14)
EARLY_INVERT = (1, 2, 7, 13)
BESIDE = {
    1: [("out", 1, 1)],
    2: [("centre", 7)],
    3: [("average", 7), ("normed", 7)],
    4: [("logits", 1), ("routing", 1)],
    6: [("comb", 1)],
}


def build_program(nc, xT, ctxT, wqkv, woq, cols, mix, bv, gate_b, wexp, wcon, eup, edn, gu, gus, w2p, w2s,
                  gwT, consts, sel, fixed, outT):
    f32, bf16, u16, u32 = mybir.dt.float32, mybir.dt.bfloat16, mybir.dt.uint16, mybir.dt.uint32
    ACT, ALU, AX = mybir.ActivationFunctionType, mybir.AluOpType, mybir.AxisListType
    bounce = nc.dram_tensor("bounce", [4 * LAYERS, len(TERMS_Q), D, CH], bf16).ap()

    with ExitStack() as ctx:
        def sb(name, shape, dt=f32):
            return ctx.enter_context(nc.sbuf_tensor(name, shape, dt))

        def pb(name, shape):
            return ctx.enter_context(nc.psum_tensor(name, shape, f32))

        def sem(name):
            return ctx.enter_context(nc.semaphore(name))

        eps = sb("eps", [D, 1])
        x = sb("x", [D, TOK])
        cx = sb("cx", [D, TOK])
        xn = sb("xn", [D, TOK])
        w_qkv = sb("w_qkv", [D, LAYERS, 3, D])
        w_o = sb("w_o", [D, LAYERS, 4, D])
        col = sb("col", [D, 13])
        mixc = sb("mixc", [D, 4, 2, 2, 2])
        bvb = sb("bvb", [D, LAYERS, D])
        gbb = sb("gbb", [D, EXPERTS])
        cst = sb("cst", [D, 3, D])
        selt = sb("selt", [80, EPAIRS, D], bf16)
        K = sb("K", [D, 2, PAIRS, TOK], bf16)
        Q = sb("Q", [D, PAIRS, TOK], bf16)
        V = sb("V", [D, 2 * BATCH, HEADS, 32])
        terms = sb("terms", [D, 2, 3, CH], bf16)
        rest = sb("rest", [D, 2, CH])
        P = sb("P", [D, 4, 2, 2, SEQ])
        attn = sb("attn", [D, 4, TOK])
        nm = sb("nm", [D, 2, 2, 8])
        nm2 = sb("nm2", [D, 2, 32])
        nm_hi = sb("nm_hi", [16, 2, SEQ], bf16)
        nmT = sb("nmT", [16, 2, SEQ], bf16)
        o_raw = sb("o_raw", [D, 2, CH])
        sums = sb("sums", [D, 2, CH])
        rinv = sums
        sq = sb("sq", [D, 2, CH])
        rstd = sb("rstd", [D, 2, CH])
        w_exp = sb("w_exp", [D, BLK, D + 1])
        w_con = sb("w_con", [D, BLK, D])
        e_up = sb("e_up", [D, BLK, EDGE])
        e_dn = sb("e_dn", [D, BLK, EDGE])
        g_up = sb("g_up", [D, BLK, D + 1])
        mix_a = sb("mix_a", [D, BLK, D + 1])
        mix_b = sb("mix_b", [D, BLK, D + 1])
        w_up = sb("w_up", [D, BLK, D])
        w_dn = sb("w_dn", [D, BLK, D])
        b_up = sb("b_up", [D, BLK])
        b_dn = sb("b_dn", [D, 1])
        w_gu = sb("w_gu", [D, EPAIRS, 2, D])
        w_2 = sb("w_2", [D, EPAIRS, D])
        w_gus = sb("w_gus", [D, 2 * INTER])
        w_2s = sb("w_2s", [D, D])
        w_g = sb("w_g", [D, EXPERTS])
        route = sb("route", [D, 8, 4, EXPERTS])
        top = sb("top", [D, 4, 8])
        rsum = sb("rsum", [D, 2, 4])
        crest = sb("crest", [EXPERTS, CH])
        cterm = sb("cterm", [EXPERTS, 2, CH], bf16)
        combT = sb("combT", [80, 2, CH], bf16)
        gate_t = sb("gate_t", [D, 2, CH])
        prod_t = sb("prod_t", [D, 2, CH])
        hid_t = sb("hid_t", [D, 2, CH])

        SB = pb("SB", [D, 2, 2, CH])
        MB = pb("MB", [D, 2, CH])
        OB = pb("OB", [D, CH])
        GB = pb("GB", [D, CH])

        x_in = [sem(f"x_in{c}") for c in range(NCH)]
        cx_in = [sem(f"cx_in{c}") for c in range(NCH)]
        cst_in, wqkv_in, col_in, bv_in = sem("cst_in"), sem("wqkv_in"), sem("col_in"), sem("bv_in")
        ffn_in, wo_in, moe_in, fixed_in = sem("ffn_in"), sem("wo_in"), sem("moe_in"), sem("fixed_in")
        eps_set, k_zero0, k_zero1, v_ones, comb_zero = (sem(n) for n in (
            "eps_set", "k_zero0", "k_zero1", "v_ones", "comb_zero"))
        gb_made, gb_read = sem("gb_made"), sem("gb_read")
        squared, rstd_done, xn_done = sem("squared"), sem("rstd_done"), sem("xn_done")
        k_projected, k_read, split_done = (sem(n) for n in ("k_projected", "k_read", "split_done"))
        bounced = [sem(f"bounced{m}") for m in range(4 * LAYERS)]
        stacked = [sem(f"stacked{m}") for m in range(4 * LAYERS)]
        v_mm, v_done = sem("v_mm"), sem("v_done")
        max_mm, max_red, doubled = sem("max_mm"), sem("max_red"), sem("doubled")
        shift_in = [sem(f"shift_in{i}") for i in range(2)]
        scored, exp_done, pv_done, spread, o_copied, o_logged, o_rinv, attn_done = (sem(n) for n in (
            "scored", "exp_done", "pv_done", "spread", "o_copied", "o_logged", "o_rinv", "attn_done"))
        fw_pool, b_built = sem("fw_pool"), sem("b_built")
        up_mm, gelu_done = sem("up_mm"), sem("gelu_done")
        comb_done, combT_done = sem("comb_done"), sem("combT_done")
        gate_mm, silu_done, prod_done, hid_done = sem("gate_mm"), sem("silu_done"), sem("prod_done"), sem("hid_done")
        hid_used, moe_added = sem("hid_used"), sem("moe_added")
        dve_self, pool_self = sem("dve_self"), sem("pool_self")
        stored = sem("stored")

        KEY_BANKS = (OB[:, :], MB[:, 0, :])
        UP_BANKS = (SB[:, 0, 0, :], SB[:, 0, 1, :], OB[:, :], GB[:, :])

        def chunk(c):
            return slice(c * CH, (c + 1) * CH)

        PROJ = [(0, 1, 0), (0, 0, 0), (0, 1, 1), (0, 0, 1), (1, 1, 0), (1, 0, 0), (1, 1, 1), (1, 0, 1)]
        NORM = [(0, 0), (0, 1), (1, 0), (2, 0), (1, 1), (2, 1), (3, 0), (3, 1)]

        def unit(U):
            l, u = divmod(U, UPL)
            return l, u // 2, u % 2

        def queries(b):
            return slice(b * SEQ, (b + 1) * SEQ)

        PLAN = {(U, k): [] for U in range(UNITS + 1) for k in range(-1, 4)}
        for U in range(UNITS):
            later = U + 2 if U + 2 < UNITS and U + 2 not in PLACED else None
            for k in range(4):
                m = maxima(later, 2 * k, 2 * k + 1) if later else []
                steps = PLAN[U, k]
                steps += EXTRA.get((U, k, "first"), []) + m[0:1] + EXTRA.get((U, k, "early"), [])
                if k == 1 and U and U not in FLUSHED:
                    steps += [("weighted", U - 1, 1)]
                if k == 3:
                    steps += [("weighted", U, 0)]
                if k == 1 and U in LATE_TURN:
                    steps += [("turn", U + 1)]
                steps += m[1:]
                if k == 0 and U not in LATE_TURN and U + 1 < UNITS and U + 1 not in FLUSHED:
                    steps += [("turn", U + 1)]
                if k == (1 if U in EARLY_INVERT else 2) and U and U not in FLUSHED:
                    steps += [("invert", U - 1)]
                steps += EXTRA.get((U, k, "late"), [])
        for U in FLUSHED + (UNITS,):
            PLAN[U, -1] += [("weighted", U - 1, 1), ("invert", U - 1)] + EXTRA.get((U, -1, "late"), [])
        PLAN[0, -1] += EXTRA[0, -1, "late"]

        def up_at(c):
            return next(point[0] for point, steps in PLAN.items() if ("up", c) in steps)

        def do_steps(steps, engine_steps):
            for step, *args in steps:
                if step in engine_steps:
                    engine_steps[step](*args)

        def do_plan(engine_steps, pair=None):
            for (U, k), steps in PLAN.items():
                if pair and U < UNITS and k >= 0:
                    pair(U, k)
                do_steps(steps, engine_steps)

        gb_no = {}

        block = ctx.enter_context(nc.Block())

        @block.tensor
        def _(pe):
            CENTRE, MEAN, EYE = (cst[:, i, :] for i in range(3))

            def mm(out, lhsT, rhs, start=True, stop=True):
                return nc.tensor.matmul(out, lhsT, rhs, start=start, stop=stop)

            def take_gb(*step):
                if gb_no:
                    pe.wait_ge(gb_read, len(gb_no))
                gb_no[step] = len(gb_no) + 1

            def centre(n):
                s, c = NORM[n]
                take_gb("centre", n)
                if s == 0:
                    pe.wait_ge(x_in[c], 16)
                    pe.wait_ge(cst_in, 16)
                mm(GB[:, :], CENTRE, x[:, chunk(c)]).then_inc(gb_made, 1)

            def average(n):
                s, c = NORM[n]
                take_gb("average", n)
                pe.wait_ge(squared, n + 1)
                mm(GB[:, :], MEAN, sq[:, c, :]).then_inc(gb_made, 1)

            def project_keys(l, c):
                if (l, c) == (0, 0):
                    pe.wait_ge(wqkv_in, 16)
                else:
                    pe.wait_ge(k_read, 2 * l + c)
                if l == 0:
                    pe.wait_ge(cx_in[c], 16)
                else:
                    pe.wait_ge(max_red, 8 * UPL)
                mm(KEY_BANKS[l], w_qkv[:, l, 1, :], cx[:, chunk(c)]).then_inc(k_projected, 1)

            def project(m):
                l, is_k, c = PROJ[m]
                if is_k:
                    project_keys(l, c)
                    return
                take_gb("project", m)
                pe.wait_ge(xn_done, NORM.index((2 * l, c)) + 1)
                mm(GB[:, :], w_qkv[:, l, 0, :], xn[:, chunk(c)]).then_inc(gb_made, 1)

            def value_products(bank, l, c):
                for t in range(4):
                    at = c * CH + t * D
                    last = mm(bank[:, D * t:D * t + D], cx[:, at:at + D], w_qkv[:, l, 2, :])
                return last

            def next_values(c):
                if c == 0:
                    pe.wait_ge(max_red, 8 * UPL)
                    value_products(MB[:, 1, :], 1, c).then_inc(v_mm, 1)
                else:
                    take_gb("values", c)
                    value_products(GB, 1, c).then_inc(gb_made, 1)

            def maxima(U, i):
                l, b, g = unit(U)
                k, qt = divmod(i, 2)
                p = 4 * g + k
                if i == 0 and U % 4 == 0:
                    c = b // 2
                    pe.wait_ge(stacked[PROJ.index((l, 1, c))], 2 * 16)
                    pe.wait_ge(stacked[PROJ.index((l, 0, c))], (2 + 2 * l) * 16)
                    if U == 0:
                        pe.wait_ge(fixed_in, 4 * 16)
                        pe.wait_ge(k_zero0, 2)
                    if U == 4:
                        pe.wait_ge(k_zero1, 2)
                    if U == 8:
                        pe.wait_ge(k_read, 4)
                if 8 * U + i >= 2:
                    pe.wait_ge(max_red, 8 * U + i - 1)
                elif i == 0:
                    pe.wait_ge(v_done, 2)
                if U == 8 and i == 1:
                    pe.wait_ge(v_done, 3)
                q0 = b * SEQ + qt * D
                mm(MB[:, i % 2, :].rearrange("p (h s) -> p h s", h=2), Q[:, p, q0:q0 + D],
                   K[:, :, p, queries(b)]).then_inc(max_mm, 1)

            def turn(U):
                take_gb("turn", U)
                pe.wait_ge(doubled, U + 1)
                for qt in range(2):
                    last = mm(GB[0:16, D * qt:D * qt + D], nm2[:, U % 2, 16 * qt:16 * qt + 16], EYE)
                last.then_inc(gb_made, 1)

            ups = []

            def scores(U, k):
                l, b, g = unit(U)
                i = 4 * U + k
                if k == 0:
                    pe.wait_ge(shift_in[U % 2], 32 * (U // 2 + 1))
                if i >= 2:
                    pe.wait_ge(exp_done, i - 1)
                if ups and i % 2 == 0:
                    pe.wait_ge(gelu_done, 3 * len(ups))
                for kt in range(2):
                    s0 = b * SEQ + kt * D
                    for hh in range(2):
                        last = mm(SB[:, i % 2, kt, hh * SEQ:(hh + 1) * SEQ], K[:, hh, 4 * g + k, s0:s0 + D],
                                  Q[:, 4 * g + k, queries(b)])
                last.then_inc(scored, 1)

            def weighted(U, half):
                l, b, g = unit(U)
                pe.wait_ge(exp_done, 4 * U + 2 * half + 2)
                if half == 0 and U:
                    pe.wait_ge(o_copied, U)
                    if ups:
                        pe.wait_ge(gelu_done, 3 * len(ups))
                for kt in range(2):
                    for j in range(4):
                        k, hh = 2 * half + j // 2, j % 2
                        h = 2 * (4 * g + k) + hh
                        last = mm(OB[32 * j:32 * j + 32, half * SEQ:(half + 1) * SEQ], V[:, 2 * b + kt, h, :],
                                  P[:, (4 * U + k) % 4, kt, hh, :], start=kt == 0, stop=kt == 1)
                last.then_inc(pv_done, 1)

            def out_project(l, c, parts=range(4)):
                for i in parts:
                    if i == 0:
                        take_gb("out", l, c)
                        pe.wait_ge(attn_done, UPL * l + 4 * c + 4)
                        if l == 0 and c == 0:
                            pe.wait_ge(wo_in, 16)
                    last = mm(GB[:, :], w_o[:, l, i, :], attn[:, i, chunk(c)], start=i == 0, stop=i == 3)
                    if i == 3:
                        last.then_inc(gb_made, 1)

            def fw(step):
                take_gb("fw", step)
                if step == 0:
                    pe.wait_ge(fw_pool, 1)
                    for b in range(BLK):
                        last = mm(GB[:, D * b:D * b + D], e_up[:, b, EDGE - D:EDGE], w_exp[:, b, 0:D])
                elif step == 1:
                    for b in range(BLK):
                        last = mm(GB[:, b:b + 1], e_up[:, b, EDGE - D:EDGE], w_exp[:, b, D:D + 1])
                elif step == 2:
                    pe.wait_ge(fw_pool, 2)
                    for b in range(BLK):
                        last = mm(GB[:, D * b:D * b + D], e_dn[:, b, EDGE - D:EDGE], w_con[:, b, :])
                else:
                    pe.wait_ge(fw_pool, 3)
                    for b in range(BLK):
                        last = mm(GB[:, D * b:D * b + D], g_up[:, b, 0:D], EYE)
                last.then_inc(gb_made, 1)

            def up(c):
                take_gb("up", c)
                pe.wait_ge(xn_done, NORM.index((1, c)) + 1)
                pe.wait_ge(exp_done, 4 * up_at(c) + 3)
                for k in range(BLK):
                    if k == 2:
                        pe.wait_ge(o_copied, up_at(c))
                    mm(UP_BANKS[k], w_up[:, k, :], xn[:, chunk(c)])\
                        .then_inc(up_mm if k < BLK - 1 else gb_made, 1)
                ups.append(c)

            def down(c):
                take_gb("down", c)
                pe.wait_ge(gelu_done, 3 * c + 3)
                for k in range(BLK):
                    last = mm(GB[:, :], w_dn[:, k, :], attn[:, k, chunk(c)], start=k == 0, stop=k == BLK - 1)
                last.then_inc(gb_made, 1)

            def router_logits(c):
                take_gb("logits", c)
                pe.wait_ge(moe_in, 7 * 16)
                pe.wait_ge(xn_done, NORM.index((3, c)) + 1)
                for t in range(4):
                    at = c * CH + t * D
                    last = mm(GB[:, 16 * t:16 * t + 16], xn[:, at:at + D], w_g[:, :])
                last.then_inc(gb_made, 1)

            def turn_weights(c):
                take_gb("comb", c)
                pe.wait_ge(comb_done, c + 1)
                for t in range(4):
                    last = mm(GB[0:16, D * t:D * t + D], route[:, 6 + c, t, :], EYE)
                last.then_inc(gb_made, 1)

            steps = {"centre": centre, "average": average, "project": project, "values": next_values,
                     "out": out_project, "fw": fw, "up": up, "down": down, "logits": router_logits,
                     "comb": turn_weights, "maximum": maxima, "turn": turn, "weighted": weighted}

            centre(0)
            project(0)
            average(0)
            project(1)
            project(2)
            centre(1)
            for c in range(NCH):
                value_products(MB[:, c, :], 0, c).then_inc(v_mm, 1)
            average(1)
            pe.wait_ge(k_read, 2)
            do_plan(steps, scores)

            pe.wait_ge(exp_done, 4 * UPL * LAYERS)
            pe.wait_ge(max_red, 8 * UPL * LAYERS)

            for c in range(NCH):
                pe.wait_ge(combT_done, 2 * (c + 1))

                def down_product(e):
                    i = (EPAIRS + 1) * c + e
                    rows = D if e < EPAIRS else INTER
                    if i == 0:
                        pe.wait_ge(o_copied, UPL * LAYERS)
                    if e == 0 and c:
                        pe.wait_ge(moe_added, c)
                    if e < EPAIRS:
                        pe.wait_ge(hid_done, EPAIRS * c + e + 1)
                    else:
                        pe.wait_ge(prod_done, i + 1)
                    w = w_2[:, e, :] if e < EPAIRS else w_2s[INTER:D, :]
                    mm(OB[:, :], w, hid_t[D - rows:D, i % 2, :], start=e == 0, stop=e == EPAIRS).then_inc(hid_used, 1)

                for e in range(EPAIRS + 1):
                    i = (EPAIRS + 1) * c + e
                    if i >= 2:
                        pe.wait_ge(prod_done, i - 1)
                        pe.wait_ge(hid_done, EPAIRS * c + e - 1 if e else EPAIRS * c)
                    for j in range(2 if e < EPAIRS else 1):
                        w = w_gu[:, e, j, :] if e < EPAIRS else w_gus[:, :]
                        last = mm(SB[:, i % 2, j, :], w, xn[:, chunk(c)])
                    if e < EPAIRS:
                        last = mm(MB[:, i % 2, :], selt[:, e, :], combT[:, c, :])
                    last.then_inc(gate_mm, 1)
                    if c == 0:
                        do_steps(BESIDE.get(e, ()), steps)
                    if e:
                        down_product(e - 1)
                down_product(EPAIRS)

        @block.sync
        def _(sp):
            def send_terms(m):
                is_k = PROJ[m][1]
                t = terms[:, m % 2, :, :]
                if is_k:
                    parts = ((5, 6, t[:, 0:1, :]), (3, 5, t[:, 0:2, :]), (0, 3, t))
                else:
                    parts = ((0, 3, t[:, 0:1, :].broadcast_to([D, 3, CH])),
                             (3, 5, t[:, 1:2, :].broadcast_to([D, 2, CH])), (5, 6, t[:, 2:3, :]))
                for i, (t0, t1, src) in enumerate(parts):
                    sp.wait_ge(split_done, 3 * m + i + 1)
                    sp.dma_start(bounce[m, t0:t1, :, :].rearrange("t r n -> r t n"), src).then_inc(bounced[m], 16)

            def stack(m):
                l, is_k, c = PROJ[m]
                sp.wait_ge(bounced[m], 48)
                if l:
                    sp.wait_ge(scored, 4 * 4 * (c + 1))
                for hh in range(2):
                    dst = K[64 * hh:64 * hh + SHIFT, hh, :, chunk(c)] if is_k \
                        else Q[64 * hh:64 * hh + SHIFT, :, chunk(c)]
                    src = bounce[m, :, 64 * hh:64 * hh + 64, :].rearrange("t (d p) n -> t d p n", d=DH)
                    sp.dma_start(dst, src).then_inc(stacked[m], 16)
                if l and not is_k:
                    for hh in range(2):
                        sp.dma_start(Q[64 * hh + SHIFT:64 * hh + SHIFT + 2, :, chunk(c)].bitcast(u16),
                                     fixed[1, 0:PAIRS * CH].rearrange("(p n) -> p n", p=PAIRS)
                                     .partition_broadcast(2)).then_inc(stacked[m], 16)

            def shift_rows(U):
                l, b, g = unit(U)
                sp.wait_ge(gb_read, gb_no["turn", U])
                for hh in range(2):
                    rows = slice(64 * hh + SHIFT, 64 * hh + SHIFT + 2)
                    sp.dma_start(Q[rows, 4 * g:4 * g + 4, queries(b)], nmT[8 * hh:8 * hh + 8, U % 2, :])\
                        .then_inc(shift_in[U % 2], 16)

            sp.dma_start(x[:, chunk(0)], xT[:, chunk(0)]).then_inc(x_in[0], 16)
            sp.dma_start(cx[:, chunk(0)], ctxT[:, chunk(0)]).then_inc(cx_in[0], 16)
            sp.dma_start(x[:, chunk(1)], xT[:, chunk(1)]).then_inc(x_in[1], 16)
            sp.dma_start(cx[:, chunk(1)], ctxT[:, chunk(1)]).then_inc(cx_in[1], 16)
            for hh in range(2):
                sp.dma_start(K[64 * hh + SHIFT:64 * hh + 64, hh, :, :].bitcast(u16),
                             fixed[0].rearrange("(p n) -> p n", p=PAIRS).partition_broadcast(64 - SHIFT))\
                    .then_inc(fixed_in, 16)
                sp.dma_start(Q[64 * hh + SHIFT:64 * hh + 64, :, :].bitcast(u16),
                             fixed[1].rearrange("(p n) -> p n", p=PAIRS).partition_broadcast(64 - SHIFT))\
                    .then_inc(fixed_in, 16)
            sp.dma_start(bvb[:, :, :], bv.rearrange("l d -> (l d)").partition_broadcast(D)).then_inc(bv_in, 16)
            send_terms(0)
            send_terms(1)
            stack(0)
            stack(1)
            send_terms(2)
            stack(2)
            do_plan({"split": send_terms, "stack": stack, "turn": shift_rows})
            for c in range(NCH):
                sp.wait_ge(moe_added, c + 1)
                sp.dma_start(outT[:, chunk(c)], x[:, chunk(c)]).then_inc(stored, 16)
            sp.wait_ge(stored, 16 * NCH)

        @block.gpsimd
        def _(pool):
            steps = [0]

            def link(ins):
                steps[0] += 1
                ins.then_inc(pool_self, 1)
                pool.wait_ge(pool_self, steps[0])

            for hh in range(2):
                nc.gpsimd.memset(K[64 - 64 * hh:128 - 64 * hh, hh, :, chunk(1)].bitcast(u32), 0).then_inc(k_zero1, 1)
                pool.wait_ge(k_zero1, hh + 1)
            nc.gpsimd.memset(V[:, :, :, DH:32], 1.0).then_inc(v_ones, 1)
            pool.wait_ge(v_ones, 1)
            nc.gpsimd.memset(combT[:, :, :].bitcast(u32), 0).then_inc(comb_zero, 1)
            pool.wait_ge(comb_zero, 1)
            pool.wait_ge(stacked[1], 2 * 16)
            for dst, src in ((e_up[:, :, :], eup), (e_dn[:, :, :], edn), (mixc[:, :, :, :, :], mix),
                             (w_exp[:, :, :], wexp), (w_con[:, :, :], wcon)):
                pool.dma_start(dst, src).then_inc(ffn_in, 16)
            pool.dma_start(w_o[:, :, :, :], woq).then_inc(wo_in, 16)

            pool.wait_ge(ffn_in, 5 * 16)
            for s in range(1, 7):
                w = 2 ** s
                at = 2 * w - 2
                old = e_up[:, :, at - w:at].unsqueeze(2).broadcast_to([D, BLK, 2, w])
                new = e_up[:, :, at:at + 2 * w].rearrange("p b (o i) -> p b o i", o=2)
                link(nc.gpsimd.tensor_tensor(new, new, old, ALU.mult))
            for s in range(1, 7):
                w = 2 ** s
                at = 2 * w - 2
                old = e_dn[:, :, at - w:at].unsqueeze(3).broadcast_to([D, BLK, w, 2])
                new = e_dn[:, :, at:at + 2 * w].rearrange("p b (i o) -> p b i o", o=2)
                ins = nc.gpsimd.tensor_tensor(new, new, old, ALU.mult)
                if s < 6:
                    link(ins)
            ins.then_inc(fw_pool, 1)

            def mix_blocks(k, low, dst, src, n):
                s4 = src.rearrange("p (h l) n -> p h l n", h=2)
                d4 = dst.rearrange("p (h l) n -> p h l n", h=2)
                for i, t in ((0, mix_a), (1, mix_b)):
                    s = s4[:, :, i:i + 1, :] if low else s4[:, i:i + 1, :, :]
                    t4 = t[:, :, 0:n].rearrange("p (h l) n -> p h l n", h=2)
                    cc = mixc[:, k, :, :, i:i + 1].broadcast_to([D, 2, 2, n])
                    ins = nc.gpsimd.tensor_tensor(t4, s.broadcast_to([D, 2, 2, n]), cc, ALU.mult)
                    link(ins)
                return nc.gpsimd.tensor_tensor(d4, mix_a[:, :, 0:n].rearrange("p (h l) n -> p h l n", h=2),
                                               mix_b[:, :, 0:n].rearrange("p (h l) n -> p h l n", h=2), ALU.add)

            link(mix_blocks(2, False, w_con[:, :, :], w_con[:, :, :], D))
            mix_blocks(3, True, w_con[:, :, :], w_con[:, :, :], D).then_inc(fw_pool, 1)

            def normalise(U):
                l, b, g = unit(U)
                pool.wait_ge(o_rinv, U + 1)
                if l and U % 4 == 0:
                    pool.wait_ge(gb_read, gb_no["down", b // 2])
                nc.gpsimd.tensor_tensor(attn[:, 2 * g:2 * g + 2, queries(b)],
                                        o_raw[:, U % 2, :].rearrange("p (h q) -> p h q", h=2),
                                        rinv[:, U % 2, :].rearrange("p (h q) -> p h q", h=2),
                                        ALU.mult).then_inc(attn_done, 1)

            def load_experts():
                for dst, src in ((w_gu[:, :, :, :], gu), (w_2[:, :, :], w2p),
                                 (w_gus[:, :], gus), (w_2s[INTER:D, :], w2s),
                                 (w_g[:, :], gwT), (selt[:, :, :].bitcast(u16), sel),
                                 (gbb[:, :], gate_b.partition_broadcast(D))):
                    pool.dma_start(dst, src).then_inc(moe_in, 16)

            def mix_up():
                pool.wait_ge(gb_read, gb_no["fw", 1])
                pool.wait_ge(fw_pool, 2)
                link(mix_blocks(0, True, g_up[:, :, :], g_up[:, :, :], D + 1))
                mix_blocks(1, False, g_up[:, :, :], g_up[:, :, :], D + 1).then_inc(fw_pool, 1)

            def after_weighted(U, half):
                if half:
                    normalise(U)
                    if U == 1:
                        mix_up()
                        load_experts()

            do_plan({"weighted": after_weighted})

        @block.scalar
        def _(act):
            act.dma_start(cst[:, :, :], consts).then_inc(cst_in, 16)
            act.dma_start(w_qkv[:, :, :, :], wqkv).then_inc(wqkv_in, 16)
            act.dma_start(col[:, :], cols).then_inc(col_in, 16)

            def square(n):
                c = NORM[n][1]
                act.wait_ge(gb_made, gb_no["centre", n])
                nc.scalar.activation(sq[:, c, :], GB[:, :], ACT.Square).then_inc(squared, 1)
                nc.scalar.activation(xn[:, chunk(c)], GB[:, :], ACT.Copy).then_inc(gb_read, 1)

            def rstd_of(n):
                c = NORM[n][1]
                act.wait_ge(gb_made, gb_no["average", n])
                nc.scalar.activation(rstd[:, c, :], GB[:, :], ACT.Ln, bias=eps[:, 0:1]).then_inc(gb_read, 1)
                act.wait_ge(gb_read, gb_no["average", n])
                nc.scalar.activation(rstd[:, c, :], rstd[:, c, :], ACT.Exp, scale=-0.5).then_inc(rstd_done, 1)

            def exps(U, k):
                i = 4 * U + k
                act.wait_ge(scored, i + 1)
                if i >= 4:
                    act.wait_ge(pv_done, (i - 4) // 2 + 1)
                nc.scalar.activation(P[:, i % 4, :, :, :].rearrange("p k h q -> p (k h q)"),
                                     SB[:, i % 2, :, :].rearrange("p k n -> p (k n)"),
                                     ACT.Exp, scale=SCALE).then_inc(exp_done, 1)

            def invert(U):
                act.wait_ge(spread, U + 1)
                if U >= 2:
                    act.wait_ge(attn_done, U - 1)
                nc.scalar.activation(o_raw[:, U % 2, :], OB[:, :], ACT.Copy).then_inc(o_copied, 1)
                nc.scalar.activation(rinv[:, U % 2, :], sums[:, U % 2, :], ACT.Ln).then_inc(o_logged, 1)
                act.wait_ge(o_logged, U + 1)
                nc.scalar.activation(rinv[:, U % 2, :], rinv[:, U % 2, :], ACT.Exp, scale=-1.0).then_inc(o_rinv, 1)

            def gelu(c):
                act.preload_act_table_set(GELU)
                for k in range(BLK):
                    if k < BLK - 1:
                        act.wait_ge(up_mm, 3 * c + k + 1)
                    else:
                        act.wait_ge(gb_made, gb_no["up", c])
                    nc.scalar.activation(attn[:, k, chunk(c)], UP_BANKS[k], ACT.Gelu,
                                         bias=b_up[:, k:k + 1]).then_inc(gelu_done if k < BLK - 1 else gb_read, 1)
                act.preload_act_table_set(EXP_LN)

            def router_exp(c):
                act.wait_ge(gb_made, gb_no["logits", c])
                nc.scalar.activation(route[:, c, :, :], GB[:, 0:64].rearrange("p (t e) -> p t e", e=EXPERTS),
                                     ACT.Exp, scale=-1.0).then_inc(gb_read, 1)

            steps = {"centre": square, "average": rstd_of, "up": gelu, "logits": router_exp,
                     "invert": invert}

            act.preload_act_table_set(EXP_LN)
            act.wait_ge(eps_set, 1)
            square(0)
            rstd_of(0)
            square(1)
            rstd_of(1)
            do_plan(steps, exps)

            def rstd_beside(n):
                act.preload_act_table_set(EXP_LN)
                rstd_of(n)

            def exp_beside(c):
                router_exp(c)
                act.preload_act_table_set(SILU)

            steps = {"centre": square, "average": rstd_beside, "logits": exp_beside}
            for c in range(NCH):
                for e in range(EPAIRS + 1):
                    i = (EPAIRS + 1) * c + e
                    rows = D if e < EPAIRS else INTER
                    if i == 0:
                        act.preload_act_table_set(SILU)
                    act.wait_ge(gate_mm, i + 1)
                    if i >= 2:
                        act.wait_ge(prod_done, i - 1)
                    nc.scalar.activation(gate_t[D - rows:D, i % 2, :], SB[0:rows, i % 2, 0, :], ACT.Silu)\
                        .then_inc(silu_done, 1)
                    if c == 0:
                        do_steps(BESIDE.get(e, ()), steps)

        @block.vector
        def _(dve):
            links = [0]

            def link(ins):
                links[0] += 1
                ins.then_inc(dve_self, 1)
                dve.wait_ge(dve_self, links[0])

            def split(m):
                l, is_k, c = PROJ[m]
                bank = KEY_BANKS[l] if is_k else GB[:, :]
                bias = col[:, (BK if is_k else BQ) + l:(BK if is_k else BQ) + l + 1]
                t = terms[:, m % 2, :, :]
                r = rest[:, m % 2, :]
                if is_k:
                    dve.wait_ge(k_projected, 2 * l + c + 1)
                else:
                    dve.wait_ge(gb_made, gb_no["project", m])
                if m == 0:
                    dve.wait_ge(col_in, 16)
                if m >= 2:
                    dve.wait_ge(bounced[m - 2], 48)
                nc.vector.tensor_scalar(t[:, 0, :], bank, bias, None, ALU.add).then_inc(split_done, 1)
                dve.wait_ge(split_done, 3 * m + 1)
                read = nc.vector.scalar_tensor_tensor(r, bank, bias, t[:, 0, :], ALU.add, ALU.subtract)
                if is_k:
                    read.then_inc(k_read, 1)
                    dve.wait_ge(k_read, 2 * l + c + 1)
                else:
                    read.then_inc(gb_read, 1)
                    dve.wait_ge(gb_read, gb_no["project", m])
                nc.vector.tensor_copy(t[:, 1, :], r).then_inc(split_done, 1)
                dve.wait_ge(split_done, 3 * m + 2)
                nc.vector.tensor_tensor(t[:, 2, :], r, t[:, 1, :], ALU.subtract).then_inc(split_done, 1)

            def normed(n):
                c = NORM[n][1]
                dve.wait_ge(rstd_done, n + 1)
                nc.vector.tensor_tensor(xn[:, chunk(c)], xn[:, chunk(c)], rstd[:, c, :], ALU.mult).then_inc(xn_done, 1)

            def add_value_bias(l, c, bank):
                bias = bvb[:, l, :].rearrange("p (h d) -> p h d", d=DH)
                for t in range(4):
                    last = nc.vector.tensor_tensor(V[:, 4 * c + t, :, 0:DH],
                                                   bank[:, D * t:D * t + D].rearrange("p (h d) -> p h d", d=DH),
                                                   bias, ALU.add)
                return last

            def first_values(c):
                dve.wait_ge(v_mm, c + 1)
                if c == 0:
                    dve.wait_ge(bv_in, 16)
                    dve.wait_ge(v_ones, 1)
                add_value_bias(0, c, MB[:, c, :]).then_inc(v_done, 1)

            def next_values(c):
                dve.wait_ge(pv_done, 2 * 4 * (c + 1))
                if c == 0:
                    dve.wait_ge(v_mm, 3)
                    add_value_bias(1, c, MB[:, 1, :]).then_inc(v_done, 1)
                else:
                    dve.wait_ge(gb_made, gb_no["values", c])
                    add_value_bias(1, c, GB).then_inc(gb_read, 1)

            def reduce(U, i):
                k, qt = divmod(i, 2)
                dve.wait_ge(max_mm, 8 * U + i + 1)
                nc.vector.tensor_reduce(nm[:, U % 2, qt, k:8:4], MB[:, i % 2, :].rearrange("p (h s) -> p h s", h=2),
                                        AX.X, ALU.max, negate=True).then_inc(max_red, 1)
                if i == 7:
                    dve.wait_ge(max_red, 8 * (U + 1))
                    nc.vector.tensor_copy(
                        nm2[:, U % 2, :].rearrange("p (h t k) -> p h t k", h=4, t=2),
                        nm[:, U % 2, :, :].rearrange("p q (h k) -> p (q h) k", k=4).unsqueeze(2)
                        .broadcast_to([D, 4, 2, 4])).then_inc(doubled, 1)

            def split_max(U):
                dve.wait_ge(gb_made, gb_no["turn", U])
                if U >= 2:
                    dve.wait_ge(shift_in[U % 2], 32 * (U // 2))
                link(nc.vector.tensor_copy(nm_hi[:, U % 2, :], GB[0:16, 0:SEQ]))
                nc.vector.scalar_tensor_tensor(nmT[:, U % 2, :], nm_hi[:, U % 2, :], col[0:16, SECOND:SECOND + 1],
                                               GB[0:16, 0:SEQ], ALU.mult, ALU.add).then_inc(gb_read, 1)

            def spread_sums(U):
                dve.wait_ge(pv_done, 2 * (U + 1))
                if U >= 2:
                    dve.wait_ge(attn_done, U - 1)
                nc.vector.stream_shuffle(sums[:, U % 2, :], OB[:, :], [DH] * 32).then_inc(spread, 1)

            def residual(c, bias, *step):
                dve.wait_ge(gb_made, gb_no[step])
                nc.vector.scalar_tensor_tensor(x[:, chunk(c)], GB[:, :], bias, x[:, chunk(c)],
                                               ALU.add, ALU.add).then_inc(gb_read, 1)

            def add_attention(l, c, parts=(3,)):
                if 3 in parts:
                    residual(c, col[:, BO + l:BO + l + 1], "out", l, c)

            def add_ffn(c):
                dve.wait_ge(b_built, 1)
                residual(c, b_dn[:, 0:1], "down", c)

            def fw_read(step):
                dve.wait_ge(gb_made, gb_no["fw", step])
                if step == 1:
                    dst, src = g_up[:, :, D:D + 1], GB[:, 0:BLK].unsqueeze(2)
                else:
                    dst = (g_up[:, :, 0:D], None, w_dn[:, :, :], w_up[:, :, :])[step]
                    src = GB[:, :].rearrange("p (b n) -> p b n", b=BLK)
                if step == 3:
                    nc.vector.tensor_tensor(b_dn[:, :], col[:, BCON:BCON + 1], col[:, BDOWN:BDOWN + 1], ALU.add)\
                        .then_inc(b_built, 1)
                    link(nc.vector.tensor_tensor(b_up[:, :], g_up[:, :, D:D + 1].rearrange("p b o -> p (b o)"),
                                                 col[:, BUP:BUP + BLK], ALU.add))
                nc.vector.tensor_copy(dst, src).then_inc(gb_read, 1)

            def routing(c):
                ex, sc, bi, le, ws = (route[:, i, :, :] for i in (c, 2, 3, 4, 5))
                dve.wait_ge(gb_read, gb_no["logits", c])
                link(nc.vector.tensor_scalar(ex, ex, 1.0, None, ALU.add))
                link(nc.vector.reciprocal(sc, ex))
                link(nc.vector.tensor_tensor(bi, sc, gbb[:, :].unsqueeze(1).broadcast_to([D, 4, EXPERTS]), ALU.add))
                for t in range(4):
                    ins = nc.vector.max(top[:, t, :], bi[:, t, :])
                link(ins)
                link(nc.vector.memset(top[:, :, TOPK:8], -3.0e38))
                for t in range(4):
                    ins = nc.vector.match_replace(out=le[:, t, :], in_to_replace=top[:, t, :], in_values=bi[:, t, :],
                                                  imm_value=-1.0e38)
                link(ins)
                link(nc.vector.tensor_tensor(le, le, bi, ALU.not_equal))
                link(nc.vector.tensor_tensor(ws, sc, le, ALU.mult))
                link(nc.vector.reduce_sum(rsum[:, 0, :], ws, AX.X))
                link(nc.vector.reciprocal(rsum[:, 1, :], rsum[:, 0, :]))
                nc.vector.scalar_tensor_tensor(route[:, 6 + c, :, :], ws, ROUTE_SCALE,
                                               rsum[:, 1, :].unsqueeze(2).broadcast_to([D, 4, EXPERTS]),
                                               ALU.mult, ALU.mult).then_inc(comb_done, 1)

            def weight_terms(c):
                dve.wait_ge(gb_made, gb_no["comb", c])
                dve.wait_ge(comb_zero, 1)
                link(nc.vector.tensor_copy(combT[0:16, c, :], GB[0:16, :]))
                if c:
                    dve.wait_ge(combT_done, 2 * c)
                nc.vector.tensor_tensor(crest[:, :], GB[0:16, :], combT[0:16, c, :], ALU.subtract).then_inc(gb_read, 1)
                dve.wait_ge(gb_read, gb_no["comb", c])
                link(nc.vector.tensor_copy(cterm[:, 0, :], crest[:, :]))
                link(nc.vector.tensor_tensor(cterm[:, 1, :], crest[:, :], cterm[:, 0, :], ALU.subtract))
                nc.vector.tensor_copy(combT[32:48, c, :], cterm[:, 0, :]).then_inc(combT_done, 1)
                nc.vector.tensor_copy(combT[64:80, c, :], cterm[:, 1, :]).then_inc(combT_done, 1)

            def after_weighted(U, half):
                if half:
                    spread_sums(U)

            def first_routing(c):
                dve.wait_ge(moe_in, 7 * 16)
                routing(c)

            steps = {"normed": normed, "split": split, "values": next_values,
                     "out": add_attention, "fw": fw_read, "down": add_ffn, "routing": first_routing,
                     "comb": weight_terms, "maximum": reduce, "turn": split_max, "weighted": after_weighted}

            nc.vector.memset(eps[:, :], EPS).then_inc(eps_set, 1)
            for hh in range(2):
                nc.vector.memset(K[64 - 64 * hh:128 - 64 * hh, hh, :, chunk(0)].bitcast(u32), 0).then_inc(k_zero0, 1)
            split(0)
            normed(0)
            split(1)
            split(2)
            for c in range(NCH):
                first_values(c)
            normed(1)
            do_plan(steps)
            for c in range(NCH):
                for e in range(EPAIRS + 1):
                    i = (EPAIRS + 1) * c + e
                    dve.wait_ge(silu_done, i + 1)
                    if i >= 2:
                        dve.wait_ge(hid_used, i - 1)
                    rows = slice(0 if e < EPAIRS else INTER, D)
                    dst, j = (prod_t, 1) if e < EPAIRS else (hid_t, 0)
                    nc.vector.tensor_tensor(dst[rows, i % 2, :], SB[rows, i % 2, j, :], gate_t[rows, i % 2, :],
                                            ALU.mult).then_inc(prod_done, 1)
                    if e < EPAIRS:
                        dve.wait_ge(prod_done, i + 1)
                        nc.vector.tensor_tensor(hid_t[:, i % 2, :], MB[:, i % 2, :], prod_t[:, i % 2, :],
                                                ALU.mult).then_inc(hid_done, 1)
                    if c == 0:
                        do_steps(BESIDE.get(e, ()), steps)
                dve.wait_ge(hid_used, (EPAIRS + 1) * (c + 1))
                nc.vector.tensor_tensor(x[:, chunk(c)], OB[:, :], x[:, chunk(c)], ALU.add).then_inc(moe_added, 1)


_ORDER = ["xT", "ctxT", "wqkv", "woq", "cols", "mix", "bv", "gate_b", "wexp", "wcon", "eup", "edn", "gu", "gus",
          "w2p", "w2s", "gwT", "consts", "sel", "fixed"]


def _layout(inp):
    import numpy as np
    f = {k: np.asarray(v) for k, v in inp.items()}
    out = {}
    out["xT"] = f["x"].reshape(TOK, D).T
    out["ctxT"] = f["ctx_1024"].reshape(TOK, D).T
    perm = np.arange(D).reshape(PAIRS, 2, DH).transpose(1, 2, 0).reshape(-1)
    ws = []
    for l in range(LAYERS):
        q, k, v = (f[f"L{l}_xattn_W{n}"] for n in "qkv")
        if l == 0:
            q, k, v = q.T, k.T, v.T
        ws.append(np.stack([q[:, perm], k[:, perm], v], 1))
    out["wqkv"] = np.stack(ws, 1)
    wo = np.zeros((4, 32, LAYERS, 4, D), np.float32)
    for l in range(LAYERS):
        o = f[f"L{l}_xattn_Wo"]
        o = o.T if l == 0 else o
        wo[:, :DH, l] = o.reshape(4, 4, DH, D).transpose(1, 2, 0, 3)
    out["woq"] = wo.reshape(D, LAYERS, 4, D)
    vec = [f["L0_xattn_bq"][perm], f["L1_xattn_bq"][perm], f["L0_xattn_bk"][perm], f["L1_xattn_bk"][perm],
           f["L0_xattn_bo"], f["L1_xattn_bo"], f["L0_ffn_b_con"], f["L0_ffn_down_bias"]]
    vec += list(f["L0_ffn_up_bias"].reshape(BLK, D))
    vec.append(-(np.arange(D) // 4 % 2).astype(np.float32))
    out["cols"] = np.stack(vec, 1)
    up, dn = f["L0_ffn_up_weights"], f["L0_ffn_down_weights"]
    up7, dn7 = (w[7].reshape(2, D, 2, 2) for w in (up, dn))
    up8, dn8 = (w[8].reshape(2, D, 2, 2) for w in (up, dn))
    out["mix"] = np.stack([up7.transpose(1, 0, 2, 3), up8.transpose(1, 2, 0, 3),
                           dn8.transpose(1, 3, 0, 2), dn7.transpose(1, 0, 3, 2)], 1)
    out["bv"] = np.stack([f["L0_xattn_bv"], f["L1_xattn_bv"]])
    out["gate_b"] = f["L1_ffn_gate_b"]
    out["wexp"] = np.concatenate([f["L0_ffn_W_exp"].T, f["L0_ffn_b_exp"][:, None]], 1)\
        .reshape(BLK, D, D + 1).transpose(1, 0, 2)
    out["wcon"] = f["L0_ffn_W_con"].reshape(BLK, D, D).transpose(1, 0, 2)
    eu, ed = [], []
    for s in range(7):
        w = up[s].reshape(HID >> (s + 1), 2 ** s, 2, 2)
        w = w.transpose(0, 3, 2, 1).reshape(HID >> (s + 1), 2, 1, 2 ** (s + 1))
        eu.append(np.broadcast_to(w, (HID >> (s + 1), 2, 2 ** s, 2 ** (s + 1))).reshape(BLK, D, -1))
    for s in range(6, -1, -1):
        w = dn[s].reshape(BLK, 2 ** (6 - s), 2 ** s, 2, 2)
        w = w.transpose(3, 2, 0, 1, 4).reshape(1, 2 ** (s + 1), BLK, 2 ** (7 - s))
        ed.append(np.broadcast_to(w, (2 ** (6 - s), 2 ** (s + 1), BLK, 2 ** (7 - s))).reshape(D, BLK, -1))
    out["eup"] = np.concatenate(eu, 2).transpose(1, 0, 2)
    out["edn"] = np.concatenate(ed, 2)
    w13 = f["L1_ffn_w13"].reshape(EPAIRS, 2, 2, INTER, D)
    out["gu"] = w13.transpose(4, 0, 2, 1, 3).reshape(D, EPAIRS, 2, D)
    out["gus"] = f["L1_ffn_w13_s"].T
    out["w2p"] = f["L1_ffn_w2"].reshape(EPAIRS, 2, D, INTER).transpose(1, 3, 0, 2).reshape(D, EPAIRS, D)
    out["w2s"] = f["L1_ffn_w2_s"].T
    out["gwT"] = f["L1_ffn_gate_w"].T
    eye = np.eye(D, dtype=np.float32)
    mean = np.full((D, D), 1.0 / D, np.float32)
    out["consts"] = np.stack([eye - mean, mean, eye], 1)
    sel = np.zeros((3, 32, EPAIRS, 2, INTER), np.uint16)
    for e in range(EXPERTS):
        sel[:, e, e // 2, e % 2] = 0x3F80
    out["sel"] = sel.reshape(96, EPAIRS, D)[:80]
    out["fixed"] = np.repeat(np.array([0x3F80, 0], np.uint16), PAIRS * TOK).reshape(2, PAIRS * TOK)
    return {k: np.ascontiguousarray(v) for k, v in out.items()}


def kernel(**inputs):
    import numpy as np
    import concourse.bacc as bacc
    from concourse.bass_utils import run_bass_kernel_spmd

    nc = bacc.Bacc("TRN2", target_bir_lowering=False, num_devices=1)
    arrays = _layout(inputs)
    args = [nc.dram_tensor(n, arrays[n].shape, mybir.dt.from_np(arrays[n].dtype), kind="ExternalInput").ap()
            for n in _ORDER]
    args.append(nc.dram_tensor("outT", (D, TOK), mybir.dt.float32, kind="ExternalOutput").ap())
    build_program(nc, *args)
    r = run_bass_kernel_spmd(nc, [arrays], core_ids=[0])
    return np.ascontiguousarray(np.asarray(r.results[0]["outT"]).T).reshape(BATCH, SEQ, D)
```
